# Optimizing a Trainium2 kernel written in Bass

```python
import numpy as np
import jax
import jax.numpy as jnp

def _softmax(x, axis=-1):
    return jax.nn.softmax(x, axis=axis)

def _gelu(x):
    return jax.nn.gelu(x, approximate=True)

def _silu(x):
    return jax.nn.silu(x)

def _sigmoid(x):
    return jax.nn.sigmoid(x)

def _layernorm(x, axis=-1, eps=1e-05):
    m = jnp.mean(x, axis=axis, keepdims=True)
    v = jnp.var(x, axis=axis, keepdims=True)
    return (x - m) / jnp.sqrt(v + eps)

def _scatter_add(tgt, idx, src, axis=0):
    return tgt.at[idx].add(src)

def _segment_sum(src, seg, n):
    return jax.ops.segment_sum(src, seg, n)
kernel_name = 'mk_adaln_ffn_d2_seqx_r4_bd82c9'

def setup_inputs(seed: int=0):
    np.random.seed(seed)
    _w = jnp.asarray

    def _rec_inputs():
        import jax
        import jax.numpy as jnp
        _rk = jax.random.key(seed)
        x = -0.000125 + 0.9999 * jax.random.normal(jax.random.fold_in(_rk, 1), (64, 64, 1024), jnp.float32)
        _lenS = 64 - jax.random.randint(jax.random.fold_in(_rk, 7), (64,), 0, max(1, 64 // 4) + 1, jnp.int32)
        _lenS2 = 64 - jax.random.randint(jax.random.fold_in(_rk, 8), (64,), 0, max(1, 64 // 4) + 1, jnp.int32)
        cond_128 = 0.0061147 + 1.02565 * jax.random.normal(jax.random.fold_in(_rk, 11), (64, 128), jnp.float32)
        fside_S_0 = -0.022604 + 0.987366 * jax.random.normal(jax.random.fold_in(_rk, 12), (64,), jnp.float32)
        return (x, cond_128, fside_S_0)
    x, cond_128, fside_S_0 = _rec_inputs()

    def _L0_cond_setup():
        import jax, jax.numpy as jnp
        import numpy as np
        from jax import lax
        N, C_IN, L = (32, 64, 1024)
        C_OUT, K, GROUPS = (64, 9, 4)
        C_DIM, PAD, STRIDE = (128, 4, 1)
        key = jax.random.key(seed)
        k1, k2, k3, k4, k5 = jax.random.split(key, 5)
        x = jax.random.normal(k1, (N, C_IN, L), dtype=jnp.float32)
        c = jax.random.normal(k2, (N, C_DIM), dtype=jnp.float32)
        weight = jax.random.normal(k3, (C_OUT, C_IN // GROUPS, K), dtype=jnp.float32)
        c_weight = jax.random.normal(k4, (C_OUT, C_DIM), dtype=jnp.float32)
        bias = jax.random.normal(k5, (C_OUT,), dtype=jnp.float32)
        return {'x': x, 'c': c, 'weight': weight, 'c_weight': c_weight, 'bias': bias}
    _L0_cond_all = _L0_cond_setup()
    _L0_cond_in = {k: v for k, v in _L0_cond_all.items() if k in ('weight', 'c_weight')}
    del _L0_cond_all

    def _L0_ffn_setup():
        import jax, jax.numpy as jnp
        import numpy as np
        B, S, D, O, E, R = (2, 1024, 1024, 1024, 8, 16)
        TOP_K = 2
        SCALING = 32.0 / 16.0
        key = jax.random.key(seed)
        k = jax.random.split(key, 6)
        x = jax.random.normal(k[0], (B, S, D), dtype=jnp.float32)
        W_base = jax.random.normal(k[1], (O, D), dtype=jnp.float32) * 0.02
        b_base = jax.random.normal(k[2], (O,), dtype=jnp.float32) * 0.02
        W_router = jax.random.normal(k[3], (E, D), dtype=jnp.float32) * 0.01
        lora_A = jax.random.normal(k[4], (E, R, D), dtype=jnp.float32) * (1.0 / np.sqrt(D))
        lora_B = jax.random.normal(k[5], (E, O, R), dtype=jnp.float32) * 0.02
        return {'x': x, 'W_base': W_base, 'b_base': b_base, 'W_router': W_router, 'lora_A': lora_A, 'lora_B': lora_B}
    _L0_ffn_all = _L0_ffn_setup()
    _L0_ffn_in = {k: v for k, v in _L0_ffn_all.items() if k in ('W_base', 'b_base', 'W_router', 'lora_A', 'lora_B')}
    del _L0_ffn_all

    def _L1_cond_setup():
        import jax, jax.numpy as jnp
        import numpy as np
        K = 8
        T = 1.0
        D_EMBD = 128
        IN_C = 64
        OUT_C = 64
        BS = 32
        H = 1024
        HID = 128
        key = jax.random.key(seed)
        ks = jax.random.split(key, 10)
        s = lambda fan_in: 1.0 / np.sqrt(fan_in)
        return {'x': jax.random.normal(ks[0], (BS, IN_C, H), dtype=jnp.float32), 'embedding': jax.random.normal(ks[1], (BS, D_EMBD), dtype=jnp.float32), 'W0': jax.random.normal(ks[2], (D_EMBD, HID), dtype=jnp.float32) * s(D_EMBD), 'b0': jnp.zeros((HID,), dtype=jnp.float32), 'W1': jax.random.normal(ks[3], (HID, HID), dtype=jnp.float32) * s(HID), 'b1': jnp.zeros((HID,), dtype=jnp.float32), 'W2': jax.random.normal(ks[4], (HID, K), dtype=jnp.float32) * s(HID), 'b2': jnp.zeros((K,), dtype=jnp.float32), 'weight': jax.random.normal(ks[5], (K, OUT_C, IN_C, 1), dtype=jnp.float32) * s(IN_C), 'bias_k': jax.random.normal(ks[6], (K, OUT_C), dtype=jnp.float32) * 0.1}
    _L1_cond_all = _L1_cond_setup()
    _L1_cond_in = {k: v for k, v in _L1_cond_all.items() if k in ('W0', 'b0', 'W1', 'b1', 'W2', 'b2', 'weight', 'bias_k')}
    del _L1_cond_all

    def _L1_ffn_setup():
        import jax, jax.numpy as jnp
        import numpy as np
        B, S, D, O, E, R = (4, 512, 1024, 1024, 8, 16)
        SCALING = 32.0 / 16.0
        MAX_THRESHOLD = 0.125
        key = jax.random.key(seed)
        ks = jax.random.split(key, 8)
        return {'x': jax.random.normal(ks[0], (B, S, D), jnp.float32), 'W_base': jax.random.normal(ks[1], (O, D), jnp.float32) * (1.0 / np.sqrt(D)), 'b_base': jax.random.normal(ks[2], (O,), jnp.float32) * 0.02, 'W_gate': jax.random.normal(ks[3], (E, D), jnp.float32) * (1.0 / np.sqrt(D)), 'W_thr': jax.random.normal(ks[4], (D,), jnp.float32) * (1.0 / np.sqrt(D)), 'b_thr': jax.random.normal(ks[5], (1,), jnp.float32) * 0.02, 'A_w': jax.random.normal(ks[6], (E, R, D), jnp.float32) * (1.0 / np.sqrt(D)), 'B_w': jax.random.normal(ks[7], (E, O, R), jnp.float32) * (1.0 / np.sqrt(R))}
    _L1_ffn_all = _L1_ffn_setup()
    _L1_ffn_in = {k: v for k, v in _L1_ffn_all.items() if k in ('W_base', 'b_base', 'W_gate', 'W_thr', 'b_thr', 'A_w', 'B_w')}
    del _L1_ffn_all
    return {'x': x, 'cond_128': cond_128, 'fside_S_0': fside_S_0, 'L0_cond_weight': _L0_cond_in['weight'], 'L0_cond_c_weight': _L0_cond_in['c_weight'], 'L0_ffn_W_base': _L0_ffn_in['W_base'], 'L0_ffn_b_base': _L0_ffn_in['b_base'], 'L0_ffn_W_router': _L0_ffn_in['W_router'], 'L0_ffn_lora_A': _L0_ffn_in['lora_A'], 'L0_ffn_lora_B': _L0_ffn_in['lora_B'], 'L1_cond_W0': _L1_cond_in['W0'], 'L1_cond_b0': _L1_cond_in['b0'], 'L1_cond_W1': _L1_cond_in['W1'], 'L1_cond_b1': _L1_cond_in['b1'], 'L1_cond_W2': _L1_cond_in['W2'], 'L1_cond_b2': _L1_cond_in['b2'], 'L1_cond_weight': _L1_cond_in['weight'], 'L1_cond_bias_k': _L1_cond_in['bias_k'], 'L1_ffn_W_base': _L1_ffn_in['W_base'], 'L1_ffn_b_base': _L1_ffn_in['b_base'], 'L1_ffn_W_gate': _L1_ffn_in['W_gate'], 'L1_ffn_W_thr': _L1_ffn_in['W_thr'], 'L1_ffn_b_thr': _L1_ffn_in['b_thr'], 'L1_ffn_A_w': _L1_ffn_in['A_w'], 'L1_ffn_B_w': _L1_ffn_in['B_w']}

def reference(x, cond_128, fside_S_0, L0_cond_weight, L0_cond_c_weight, L0_ffn_W_base, L0_ffn_b_base, L0_ffn_W_router, L0_ffn_lora_A, L0_ffn_lora_B, L1_cond_W0, L1_cond_b0, L1_cond_W1, L1_cond_b1, L1_cond_W2, L1_cond_b2, L1_cond_weight, L1_cond_bias_k, L1_ffn_W_base, L1_ffn_b_base, L1_ffn_W_gate, L1_ffn_W_thr, L1_ffn_b_thr, L1_ffn_A_w, L1_ffn_B_w):
    import jax
    import jax.numpy as jnp

    def _L0_cond_ref(x, c, weight, c_weight, bias):
        import jax, jax.numpy as jnp
        import numpy as np
        from jax import lax
        N, C_IN, L = (32, 64, 1024)
        C_OUT, K, GROUPS = (64, 9, 4)
        C_DIM, PAD, STRIDE = (128, 4, 1)
        out = lax.conv_general_dilated(x, weight, window_strides=(STRIDE,), padding=[(PAD, PAD)], dimension_numbers=('NCH', 'OIH', 'NCH'), feature_group_count=GROUPS)
        ctx = jnp.einsum('nd,od->no', c, c_weight)
        out = out + ctx[:, :, None] + bias[None, :, None]
        return out

    def _L0_ffn_ref(x, W_base, b_base, W_router, lora_A, lora_B):
        import jax, jax.numpy as jnp
        import numpy as np
        B, S, D, O, E, R = (2, 1024, 1024, 1024, 8, 16)
        TOP_K = 2
        SCALING = 32.0 / 16.0
        d = x.shape[-1]
        n_experts = W_router.shape[0]
        xf = x.reshape(-1, d)
        logits = xf @ W_router.T
        probs = jax.nn.softmax(logits, axis=-1)
        topk_p, topk_i = jax.lax.top_k(probs, TOP_K)
        topk_p = topk_p / jnp.sum(topk_p, axis=-1, keepdims=True)
        w = jnp.sum(jax.nn.one_hot(topk_i, n_experts, dtype=xf.dtype) * topk_p[..., None], axis=1)
        h = jnp.einsum('td,erd->ter', xf, lora_A)
        lora_out = jnp.einsum('ter,eor,te->to', h, lora_B, w) * SCALING
        base = x @ W_base.T + b_base
        return base + lora_out.reshape(x.shape[:-1] + (W_base.shape[0],))

    def _L1_cond_ref(x, embedding, W0, b0, W1, b1, W2, b2, weight, bias_k):
        import jax, jax.numpy as jnp
        import numpy as np
        K = 8
        T = 1.0
        D_EMBD = 128
        IN_C = 64
        OUT_C = 64
        BS = 32
        H = 1024
        HID = 128
        h = jax.nn.gelu(embedding @ W0 + b0, approximate=False)
        h = jax.nn.gelu(h @ W1 + b1, approximate=False)
        att = jax.nn.softmax((h @ W2 + b2) / T, axis=-1)
        agg_w = jnp.einsum('bk,koi->boi', att, weight[..., 0])
        agg_b = att @ bias_k
        out = jnp.einsum('boi,bih->boh', agg_w, x) + agg_b[:, :, None]
        return out

    def _L1_ffn_ref(x, W_base, b_base, W_gate, W_thr, b_thr, A_w, B_w):
        import jax, jax.numpy as jnp
        import numpy as np
        B, S, D, O, E, R = (4, 512, 1024, 1024, 8, 16)
        SCALING = 32.0 / 16.0
        MAX_THRESHOLD = 0.125
        base = jnp.einsum('bsd,od->bso', x, W_base) + b_base
        xf = x.reshape(-1, D)
        gate = jax.nn.softmax(xf @ W_gate.T, axis=-1)
        thr = jax.nn.sigmoid(xf @ W_thr + b_thr[0]) * MAX_THRESHOLD
        adapted = gate - thr[:, None]
        selected = (adapted >= 0).astype(x.dtype)
        w = adapted * selected
        wsum = jnp.sum(w, axis=-1, keepdims=True)
        wsum = jnp.where(wsum == 0, jnp.ones_like(wsum), wsum)
        w = w / wsum
        h = jnp.einsum('nd,erd->ner', xf, A_w)
        moe = jnp.einsum('ner,ne,eor->no', h, w, B_w) * SCALING
        return base + moe.reshape(base.shape)
    x = x + _L0_ffn_ref(_L0_cond_ref(x, cond_128, L0_cond_weight, L0_cond_c_weight, fside_S_0), L0_ffn_W_base, L0_ffn_b_base, L0_ffn_W_router, L0_ffn_lora_A, L0_ffn_lora_B)
    x = x + _L1_ffn_ref(_L1_cond_ref(x, cond_128, L1_cond_W0, L1_cond_b0, L1_cond_W1, L1_cond_b1, L1_cond_W2, L1_cond_b2, L1_cond_weight, L1_cond_bias_k), L1_ffn_W_base, L1_ffn_b_base, L1_ffn_W_gate, L1_ffn_W_thr, L1_ffn_b_thr, L1_ffn_A_w, L1_ffn_B_w)
    return x

_drawn_inputs = setup_inputs


def setup_inputs(seed=0):
    import zlib

    import numpy as np

    out = dict(_drawn_inputs(seed))
    spreads = {'L1_cond_b0': (0.0, 0.1), 'L1_cond_b1': (0.0, 0.1), 'L1_cond_b2': (0.0, 0.1)}
    factors = {'L0_ffn_b_base': 23.095, 'L1_cond_bias_k': 6.517, 'L1_ffn_b_base': 39.454}
    for name, (base, spread) in spreads.items():
        noise = np.random.default_rng([zlib.crc32(name.encode()), seed]).standard_normal(out[name].shape)
        drawn = base * np.exp(spread * noise) if base else spread * noise
        out[name] = jnp.asarray(drawn.astype(out[name].dtype))
    for name, factor in factors.items():
        out[name] = (out[name] * factor).astype(out[name].dtype)
    return out
```

```python
from contextlib import ExitStack

import concourse.bass as bass
from concourse import mybir

F32 = mybir.dt.float32
F16 = mybir.dt.float16
ALU = mybir.AluOpType
ACT = mybir.ActivationFunctionType
AX = mybir.AxisListType

P = 128
NB, CH, L = 64, 64, 1024
D = CH * 2
TILES = NB // 2
KT = L // P
PH = 8
NGRP, CG, TAPS = 4, 16, 9
NNG = 2 * NGRP
BLK = L // PH + 1
BLKP = BLK + 1
EXP, RANK = 8, 16
ER = EXP * RANK
CD, HID, NK = 128, 128, 8
HALF = L // 2
G0W, G1W = ER + EXP, ER + EXP + 1
WROW = 1168

S_CONV = 4.0
S_W = 1024.0
S_AGG = 64.0
S_HW = 2.0 / S_W
PSUM0 = 1.0 / (S_CONV * S_W)
PSUM1 = 1.0 / S_W
TINY = 1.1754944e-38
MAX_THR = 0.125


def wait(eng, sem, n):
    if isinstance(n, int) and n <= 0:
        return
    eng.wait_ge(sem, n)


class Step:

    def __init__(self, j, off, known=None):
        self.j, self.off, self.known = j, off, known

    def tile(self, d=0):
        return self.known[self.off + d] if self.known else self.j * 2 + self.off + d

    def pair(self, d=0):
        return self.j + (self.off + d) // 2

    def slot(self, d=0):
        return (self.off + d) % 2

    def there(self, d=0):
        return self.known is not None or 0 <= self.tile(d) < TILES

    def is_tile(self, n, d=0):
        return self.known is None and self.tile(d) == n


def pipeline(eng, body, loop_to, reach):
    for j in (-1, 0, 1):
        for off in (0, 1):
            body(Step(j, off))
    with eng.Fori(2, loop_to) as j:
        known = {n: j * 2 + n for n in range(reach[0], reach[1] + 1)}
        for count in known.values():
            eng.compute_val(count)
        for off in (0, 1):
            body(Step(j, off, known))
    for j in range(loop_to, TILES // 2 + 1):
        for off in (0, 1):
            body(Step(j, off))


def adaln_ffn(nc, x, emb_t, fside, conv_w, cw_t, w_l0, lora_b0, b_l0, mlp_w0, mlp_b0, mlp_w1,
              mlp_b1, mlp_w2, mlp_b2, kern_w, kern_b, w_l1, lora_b1, b_l1, b_thr, out):
    with ExitStack() as ctx:
        def sb(name, shape, dt=F32, stack=ctx):
            return stack.enter_context(nc.sbuf_tensor(name, shape, dt))

        def sem(name):
            return ctx.enter_context(nc.semaphore(name))

        w0h = sb("w0h", [P, KT, WROW], F16)
        w0l = sb("w0l", [P, KT, WROW], F16)
        bh = [sb(f"b{i}h", [P, L], F16) for i in range(2)]
        bl = [sb(f"b{i}l", [P, L], F16) for i in range(2)]
        toep_h = sb("toep_h", [P, 2 * PH, CH], F16)
        toep_l = sb("toep_l", [P, 2 * PH, CH], F16)
        ctxb = sb("ctxb", [P, NB * CH])
        aggb = sb("aggb", [P, NB * CH])
        agg_t = sb("agg_t", [P, TILES, CH])
        brow = [sb(f"brow{i}", [P, L]) for i in range(2)]
        ident = sb("ident", [P, P])
        tie = sb("tie", [P, EXP, EXP])
        bthr = sb("bthr", [P, 1])
        nthr = sb("nthr", [P, 1])
        x_in = sb("x_in", [P, 2, L])
        xb = sb("xb", [P, 2, L])
        xs = sb("xs", [P, 2, PH, 2, BLKP], F16)
        xp = sb("xp", [P, 2, NNG, 2, BLKP], F16)
        act32 = sb("act32", [P, KT, D])
        yh = sb("yh", [P, KT, D], F16)
        yl = sb("yl", [P, KT, D], F16)
        zh = sb("zh", [P, KT, D], F16)
        zl = sb("zl", [P, KT, D], F16)
        x1 = sb("x1", [P, 2, L])
        x1h = sb("x1h", [P, L], F16)
        x1l = sb("x1l", [P, L], F16)
        aggh = sb("aggh", [P, D], F16)
        aggl = sb("aggl", [P, D], F16)
        stage = sb("stage", [P, 2, WROW])
        lg = sb("lg", [P, EXP + 1])
        nmax = sb("nmax", [P, 1])
        ex = sb("ex", [P, EXP])
        dif = sb("dif", [P, EXP, EXP])
        gtm = sb("gtm", [P, EXP, EXP])
        rank = sb("rank", [P, EXP])
        wsel = sb("wsel", [P, EXP])
        wsum = sb("wsum", [P, 2])
        wden = sb("wden", [P, 1])
        winv = sb("winv", [P, 2])
        thr = sb("thr", [P, 1])
        hw = sb("hw", [P, ER])
        hwh = sb("hwh", [P, D], F16)
        hwl = sb("hwl", [P, D], F16)

        with ExitStack() as pre:
            embt = sb("embt", [CD, NB], F32, pre)
            cwt = sb("cwt", [CD, CH], F32, pre)
            fsb = sb("fsb", [P, CH], F32, pre)
            fs4 = sb("fs4", [P, CH], F32, pre)
            mw0 = sb("mw0", [CD, HID], F32, pre)
            mw1 = sb("mw1", [HID, HID], F32, pre)
            mw2 = sb("mw2", [HID, NK], F32, pre)
            mb0 = sb("mb0", [HID, 1], F32, pre)
            mb1 = sb("mb1", [HID, 1], F32, pre)
            mb2 = sb("mb2", [NB, NK], F32, pre)
            h1 = sb("h1", [HID, NB], F32, pre)
            h2 = sb("h2", [HID, NB], F32, pre)
            alg = sb("alg", [NB, NK], F32, pre)
            anm = sb("anm", [NB, 1], F32, pre)
            aex = sb("aex", [NB, NK], F32, pre)
            asum = sb("asum", [NB, 1], F32, pre)
            ainv = sb("ainv", [NB, 1], F32, pre)
            att = sb("att", [NB, NK], F32, pre)
            attt = sb("attt", [NK, NB], F32, pre)
            kw = sb("kw", [NK, CH, 2, CH], F32, pre)
            kb = sb("kb", [NK, CH], F32, pre)
            ones = sb("ones", [P, P], F32, pre)
        w1h = sb("w1h", [P, KT, WROW], F16)
        w1l = sb("w1l", [P, KT, WROW], F16)

        toep = x1[:, 0, :].rearrange("p (c o) -> p c o", o=CH)
        prod = x1[:, 1, :].rearrange("p (n b o) -> p n b o", n=2, o=CH)

        acc = [ctx.enter_context(nc.psum_tensor(f"acc{i}", [P, L], F32)) for i in range(2)]
        mix = ctx.enter_context(nc.psum_tensor("mix", [P, L], F32))
        gat = ctx.enter_context(nc.psum_tensor("gat", [P, HALF], F32))
        hwt = ctx.enter_context(nc.psum_tensor("hwt", [P, HALF], F32))
        bank = [acc[0][:, 0:HALF], acc[0][:, HALF:L], acc[1][:, 0:HALF], acc[1][:, HALF:L]]

        s_toep0 = sem("s_toep0")
        s_const = sem("s_const")
        s_toep = sem("s_toep")
        s_cond = sem("s_cond")
        s_mlp = sem("s_mlp")
        s_rows = sem("s_rows")
        s_fs = sem("s_fs")
        s_toep_h = sem("s_toep_h")
        s_toep_l = sem("s_toep_l")
        s_prod = sem("s_prod")
        s_rowsum = sem("s_rowsum")
        s_rowout = sem("s_rowout")
        s_mlp_mm = sem("s_mlp_mm")
        s_mlp_act = sem("s_mlp_act")
        s_mlp_dve = sem("s_mlp_dve")
        s_attt = sem("s_attt")
        s_attt_out = sem("s_attt_out")
        s_agg = sem("s_agg")
        s_agg_out = sem("s_agg_out")
        s_stage = [sem(f"s_stage{i}") for i in range(2)]
        s_split_h = sem("s_split_h")
        s_split_l = sem("s_split_l")
        s_x = [sem(f"s_xin{i}") for i in range(2)]
        s_xh = sem("s_xh")
        s_xl = sem("s_xl")
        s_xp = [sem(f"s_xp{i}") for i in range(2)]
        s_xb = sem("s_xb")
        s_conv = sem("s_conv")
        s_y32 = sem("s_y32")
        s_yh = sem("s_yh")
        s_yl = sem("s_yl")
        s_g = [sem("s_g0"), sem("s_g1")]
        s_lg = [sem("s_lg0"), sem("s_lg1")]
        s_ex = [sem("s_ex0"), sem("s_ex1")]
        s_dve = sem("s_dve")
        s_hw = [sem("s_hw0"), sem("s_hw1")]
        s_ht = [sem("s_ht0"), sem("s_ht1")]
        s_hth = [sem("s_hth0"), sem("s_hth1")]
        s_htl = [sem("s_htl0"), sem("s_htl1")]
        s_acc = [sem("s_acc0"), sem("s_acc1")]
        s_x1 = sem("s_x1")
        s_x1h = sem("s_x1h")
        s_x1l = sem("s_x1l")
        s_x1b = sem("s_x1b")
        s_aggh = sem("s_aggh")
        s_aggl = sem("s_aggl")
        s_z = sem("s_z")
        s_z32 = sem("s_z32")
        s_zh = sem("s_zh")
        s_zl = sem("s_zl")
        s_o = sem("s_o")
        s_out = [sem(f"s_out{i}") for i in range(2)]

        pieces = []
        for src, lora_b, dst_h, dst_l, width, i in ((w_l0, lora_b0, w0h, w0l, L + G0W, 0),
                                                    (w_l1, lora_b1, w1h, w1l, L + G1W, 1)):
            for k in range(KT):
                pieces.append((src[:, k, :], dst_h[:, k, 0:width], dst_l[:, k, 0:width], width))
            pieces.append((lora_b, bh[i][:, :], bl[i][:, :], L))
        LAYER0 = KT + 1

        def by_phase(slot):
            v = x_in[:, slot, :].rearrange("p (b f) -> p f b", f=PH)
            return ((v[:, PH // 2:PH, :], 0, PH // 2, 1), (v[:, 0:PH // 2, :], PH // 2, PH, 0))

        conv_out = mix[:, :].rearrange("p (g c o) -> p g c o", g=NNG, c=PH)
        y_out = act32[:, :, :].rearrange("p c (g o) -> p g c o", g=NNG)

        def row_of(tab, n):
            return tab[:, bass.ds(n * D, D)] if not isinstance(n, int) else tab[:, n * D:(n + 1) * D]

        def agg_of(h, n):
            part = agg_t[h * CH:(h + 1) * CH, bass.ds(n, 1), :] if not isinstance(n, int) else \
                agg_t[h * CH:(h + 1) * CH, n:n + 1, :]
            return part.rearrange("p a o -> p (a o)")

        def rows(ap, n):
            return ap[bass.ds(n * D, D), :] if not isinstance(n, int) else ap[n * D:(n + 1) * D, :]

        block = ctx.enter_context(nc.Block())

        @block.sync
        def _(sp):
            def load_x(slot, n):
                sp.dma_start(x_in[:, slot, :], rows(x, n)).then_inc(s_x[slot], 16)

            load_x(0, 0)
            for dst, src in ((embt, emb_t), (cwt, cw_t)):
                sp.dma_start(dst[:, :], src).then_inc(s_cond, 16)
            sp.dma_start(fsb[:, :], fside.partition_broadcast(P)).then_inc(s_cond, 16)
            sp.wait_ge(s_toep0, 1)
            for f in range(PH):
                sp.dma_start(toep[f:P:PH, PH - 1 - f:PH - 1 - f + TAPS, :], conv_w).then_inc(s_toep, 16)
            load_x(1, 1)
            for dst, src in ((mw0[:, :], mlp_w0), (mw1[:, :], mlp_w1), (mw2[:, :], mlp_w2),
                             (mb0[:, :], mlp_b0), (mb1[:, :], mlp_b1),
                             (mb2[:, :], mlp_b2.partition_broadcast(NB)),
                             (kw[:, :, 0, :], kern_w), (kw[:, :, 1, :], kern_w),
                             (kb[:, :], kern_b)):
                sp.dma_start(dst, src).then_inc(s_mlp, 16)

            def body(s):
                if s.there(-2):
                    wait(sp, s_o, s.tile(-1))
                if s.there(3) and not s.is_tile(1, 3):
                    wait(sp, s_xb, s.tile(2))
                if s.there(2):
                    wait(sp, s_xh, s.tile(3))
                    wait(sp, s_xl, s.tile(3))
                    wait(sp, s_conv, s.tile(1))
                    for g in range(NNG):
                        sp.dma_start(xp[:, s.slot(), g, :, :].rearrange("p h b -> p (h b)"),
                                     xs[g * CG:(g + 1) * CG, s.slot(), :, :, :]
                                     .rearrange("i f h b -> i f (h b)")).then_inc(s_xp[s.slot()], 16)
                if s.there(-2):
                    sp.dma_start(rows(out, s.tile(-2)), stage[:, s.slot(), 0:L]).then_inc(s_out[s.slot()], 16)
                if s.there(3) and not s.is_tile(1, 3):
                    load_x(s.slot(3), s.tile(3))

            pipeline(sp, body, TILES // 2 - 2, (-2, 4))
            for p in range(2):
                sp.wait_ge(s_out[p], 16 * TILES // 2)

        @block.gpsimd
        def _(pool):
            nc.gpsimd.memset(toep[:, :, :], 0.0).then_inc(s_toep0, 1)
            nc.gpsimd.memset(xs[:, 0, :, :, :], 0.0).then_inc(s_const, 1)
            nc.gpsimd.memset(xs[:, 1, :, :, :], 0.0).then_inc(s_const, 1)
            nc.gpsimd.memset(ones[:, :], 1.0).then_inc(s_const, 1)
            nc.gpsimd.memset(ident[:, :], 0.0).then_inc(s_const, 1)
            nc.gpsimd.memset(tie[:, :, :], 0.0).then_inc(s_const, 1)
            nc.gpsimd.memset(aggh[:, :], 0.0).then_inc(s_const, 1)
            nc.gpsimd.memset(aggl[:, :], 0.0).then_inc(s_const, 1)
            pool.wait_ge(s_const, 7)
            nc.gpsimd.affine_select(out=ident[:, :], in_=ident[:, :], compare_op=ALU.not_equal, fill=1.0,
                                    base=0, pattern=[[-1, P]], channel_multiplier=1).then_inc(s_const, 1)
            nc.gpsimd.affine_select(out=tie[:, :, :], in_=tie[:, :, :], compare_op=ALU.is_ge, fill=-TINY,
                                    base=0, pattern=[[-1, EXP], [1, EXP]], channel_multiplier=0)\
                .then_inc(s_const, 1)

            def body(s):
                if s.there(0):
                    wait(pool, s_x1, s.tile(1))
                    wait(pool, s_x1h, s.tile(1))
                    wait(pool, s_x1l, s.tile(1))
                    if s.is_tile(0):
                        pool.wait_ge(s_rows, 16 * 3)
                    nc.gpsimd.tensor_tensor(x1[:, s.slot(), :], x1[:, s.slot(), :], brow[1][:, :], ALU.add)\
                        .then_inc(s_x1b, 1)
                if s.there(2):
                    wait(pool, s_x[s.slot()], (s.pair(2) + 1) * 16)
                    wait(pool, s_x1, s.tile(1))
                    if s.is_tile(0, 2):
                        pool.wait_ge(s_rows, 16 * 3)
                    nc.gpsimd.tensor_tensor(xb[:, s.slot(), :], x_in[:, s.slot(), :], brow[0][:, :], ALU.add)\
                        .then_inc(s_xb, 1)

            pipeline(pool, body, TILES // 2 - 1, (1, 4))

        @block.scalar
        def _(act):
            def put_stage(n):
                src, _, _, width = pieces[n]
                act.dma_start(stage[:, n % 2, 0:width], src).then_inc(s_stage[n % 2], 16)

            def split_high(n):
                _, dst, _, width = pieces[n]
                act.wait_ge(s_stage[n % 2], 16 * (n // 2 + 1))
                nc.scalar.activation(dst, stage[:, n % 2, 0:width], ACT.Copy, scale=S_W).then_inc(s_split_h, 1)
                if n + 2 < len(pieces):
                    act.wait_ge(s_split_h, n + 1)
                    act.wait_ge(s_split_l, n + 1)
                    put_stage(n + 2)

            put_stage(0)
            put_stage(1)
            act.dma_start(brow[0][:, :], b_l0.partition_broadcast(P)).then_inc(s_rows, 16)
            act.dma_start(brow[1][:, :], b_l1.partition_broadcast(P)).then_inc(s_rows, 16)
            act.dma_start(bthr[:, :], b_thr.partition_broadcast(P)).then_inc(s_rows, 16)

            def split_x(s):
                wait(act, s_x[s.slot()], (s.pair(2) + 1) * 16)
                if s.there(0):
                    wait(act, s_xp[s.slot()], (s.pair() + 1) * 16 * NNG)
                for n, (src, f0, f1, b0) in enumerate(by_phase(s.slot())):
                    a = nc.scalar.activation(xs[:, s.slot(), f0:f1, 0, b0:b0 + BLK - 1], src, ACT.Copy)
                a.then_inc(s_xh, 1)

            def prelude():
                act.wait_ge(s_toep, 16 * PH)
                nc.scalar.activation(toep_h[:, :, :], toep[:, :, :], ACT.Copy, scale=S_CONV).then_inc(s_toep_h, 1)
                act.wait_ge(s_mlp, 16 * 9)
                act.wait_ge(s_mlp_mm, 1)
                nc.scalar.activation(h1[:, :], hwt[:, 0:NB], ACT.Gelu, bias=mb0[:, 0:1]).then_inc(s_mlp_act, 1)
                act.wait_ge(s_mlp_mm, 2)
                nc.scalar.activation(h2[:, :], gat[:, 0:NB], ACT.Gelu, bias=mb1[:, 0:1]).then_inc(s_mlp_act, 1)
                act.wait_ge(s_mlp_dve, 2)
                nc.scalar.activation(aex[:, :], alg[:, :], ACT.Exp, bias=anm[:, 0:1], accum_out=asum[:, 0:1])\
                    .then_inc(s_mlp_act, 1)

            def body(s):
                if s.there(-1):
                    wait(act, s_z32, s.tile(0))
                    nc.scalar.activation(zh[:, :, :], act32[:, :, :], ACT.Copy).then_inc(s_zh, 1)
                if s.there(0):
                    wait(act, s_lg[0], s.tile(1))
                    nc.scalar.activation(ex[:, :], lg[:, 0:EXP], ACT.Exp, bias=nmax[:, 0:1])\
                        .then_inc(s_ex[0], 1)
                if s.is_tile(0):
                    for n in range(LAYER0, LAYER0 + 4):
                        split_high(n)
                if s.there(2):
                    if s.is_tile(0, 2):
                        act.wait_ge(s_const, 2)
                    split_x(s)
                if s.is_tile(-2):
                    prelude()
                if s.there(0):
                    wait(act, s_ht[0], s.tile(1))
                    nc.scalar.activation(hwh[:, :], hwt[:, 0:D], ACT.Copy, scale=S_HW).then_inc(s_hth[0], 1)
                if s.there(1):
                    wait(act, s_y32, s.tile(2))
                    nc.scalar.activation(yh[:, :, :], act32[:, :, :], ACT.Copy).then_inc(s_yh, 1)
                if s.is_tile(0, 1):
                    for n in range(LAYER0):
                        split_high(n)
                if s.there(0):
                    if s.is_tile(0):
                        act.wait_ge(s_agg_out, 4)
                        act.wait_ge(s_const, 7)
                    else:
                        wait(act, s_z, s.tile(0))
                    for h in range(2):
                        a = nc.scalar.activation(aggh[h * CH:(h + 1) * CH, h * CH:(h + 1) * CH],
                                                 agg_of(h, s.tile()), ACT.Copy, scale=S_AGG)
                    a.then_inc(s_aggh, 1)
                    wait(act, s_x1, s.tile(1))
                    nc.scalar.activation(x1h[:, :], x1[:, s.slot(), :], ACT.Copy).then_inc(s_x1h, 1)
                if s.is_tile(0):
                    for n in range(LAYER0 + 4, 2 * LAYER0):
                        split_high(n)
                if s.there(-1):
                    wait(act, s_lg[1], s.tile(0))
                    nc.scalar.activation(ex[:, :], lg[:, 0:EXP], ACT.Exp, bias=nmax[:, 0:1],
                                         accum_out=wsum[:, 0:1]).then_inc(s_ex[1], 1)
                    nc.scalar.activation(wsum[:, 1:2], lg[:, EXP:EXP + 1], ACT.Exp, scale=-1.0,
                                         bias=nthr[:, 0:1]).then_inc(s_ex[1], 1)
                    wait(act, s_ht[1], s.tile(0))
                    nc.scalar.activation(hwh[:, :], hwt[:, 0:D], ACT.Copy, scale=S_HW).then_inc(s_hth[1], 1)

            pipeline(act, body, TILES // 2 - 1, (-1, 4))

        @block.vector
        def _(dve):
            def low(dst, full, high, scale, done):
                return nc.vector.scalar_tensor_tensor(out=dst, in0=full, scalar=scale, in1=high,
                                                      op0=ALU.mult, op1=ALU.subtract).then_inc(done, 1)

            def split_low(n):
                _, high, dst, width = pieces[n]
                dve.wait_ge(s_split_h, n + 1)
                low(dst, stage[:, n % 2, 0:width], high, S_W, s_split_l)

            def context_rows(n):
                if n >= 2:
                    dve.wait_ge(s_rowsum, n - 1)
                k = n % 8
                rows_, vec, mat = (CD, embt, cwt) if n < 8 else (NK, attt, kb)
                nc.vector.tensor_tensor(
                    prod[0:rows_, n % 2, :, :],
                    vec[:, 8 * k:8 * k + 8].unsqueeze(2).broadcast_to([rows_, 8, CH]),
                    mat[:, :].unsqueeze(1).broadcast_to([rows_, 8, CH]), ALU.mult).then_inc(s_prod, 1)

            def context_out(n):
                dve.wait_ge(s_rowsum, n + 1)
                k = n % 8
                if n < 8:
                    dst = ctxb[:, k * HALF:(k + 1) * HALF].rearrange("p (b o) -> p b o", o=CH)
                    nc.vector.scalar_tensor_tensor(
                        out=dst, in0=bank[n % 4].rearrange("p (b o) -> p b o", o=CH), scalar=S_CONV,
                        in1=fs4[:, :].unsqueeze(1).broadcast_to([P, 8, CH]),
                        op0=ALU.mult, op1=ALU.add).then_inc(s_rowout, 1)
                else:
                    nc.vector.tensor_copy(aggb[:, k * HALF:(k + 1) * HALF], bank[n % 4]).then_inc(s_rowout, 1)

            def prelude():
                dve.wait_ge(s_cond, 16 * 3)
                nc.vector.tensor_scalar(fs4[:, :], fsb[:, :], S_CONV, None, ALU.mult).then_inc(s_fs, 1)
                dve.wait_ge(s_rows, 16 * 3)
                nc.vector.tensor_scalar(nthr[:, :], bthr[:, :], -1.0, None, ALU.mult).then_inc(s_fs, 1)
                context_rows(0)
                context_rows(1)
                dve.wait_ge(s_toep_h, 1)
                low(toep_l[:, :, :], toep[:, :, :], toep_h[:, :, :], S_CONV, s_toep_l)
                dve.wait_ge(s_fs, 2)
                for n in range(8):
                    context_out(n)
                    if n + 2 < 8:
                        context_rows(n + 2)
                dve.wait_ge(s_mlp, 16 * 9)
                dve.wait_ge(s_mlp_mm, 3)
                nc.vector.tensor_tensor(alg[:, :], hwt[0:NB, 256:256 + NK], mb2[:, :], ALU.add)\
                    .then_inc(s_mlp_dve, 1)
                dve.wait_ge(s_mlp_dve, 1)
                nc.vector.tensor_reduce(anm[:, :], alg[:, :], AX.X, ALU.max, negate=True).then_inc(s_mlp_dve, 1)
                dve.wait_ge(s_mlp_act, 3)
                nc.vector.reciprocal(ainv[:, :], asum[:, :]).then_inc(s_mlp_dve, 1)
                dve.wait_ge(s_mlp_dve, 3)
                nc.vector.tensor_scalar(att[:, :], aex[:, :], ainv[:, 0:1], None, ALU.mult).then_inc(s_mlp_dve, 1)
                dve.wait_ge(s_attt, 1)
                nc.vector.tensor_copy(attt[:, :], gat[0:NK, 256:256 + NB]).then_inc(s_attt_out, 1)
                dve.wait_ge(s_attt_out, 1)
                context_rows(8)
                context_rows(9)
                for n in range(8, 16):
                    context_out(n)
                    if n + 2 < 16:
                        context_rows(n + 2)
                for q in range(2):
                    for h in range(2):
                        dve.wait_ge(s_agg, 2 * q + h + 1)
                        src = acc[h][:, :].rearrange("p (o b) -> p b o", b=NB)
                        for e in range(2):
                            a = nc.vector.tensor_copy(
                                agg_t[e * CH:(e + 1) * CH, :, 32 * q + 16 * h:32 * q + 16 * h + 16],
                                src[e * CH:(e + 1) * CH, e:NB:2, :])
                        a.then_inc(s_agg_out, 1)

            def split_x(s):
                wait(dve, s_xh, s.tile(3))
                for src, f0, f1, b0 in by_phase(s.slot()):
                    a = nc.vector.tensor_tensor(xs[:, s.slot(), f0:f1, 1, b0:b0 + BLK - 1], src,
                                                xs[:, s.slot(), f0:f1, 0, b0:b0 + BLK - 1], ALU.subtract)
                a.then_inc(s_xl, 1)

            DEPTH0, DEPTH1 = 6, 9

            def gate0(s):
                t0 = s.tile() * (DEPTH0 + DEPTH1) - DEPTH1
                if s.is_tile(0):
                    t0 = 0
                wait(dve, s_g[0], s.tile(1))
                nc.vector.tensor_scalar(lg[:, 0:EXP], gat[:, ER:ER + EXP], PSUM0, None, ALU.mult)\
                    .then_inc(s_dve, 1)
                dve.wait_ge(s_dve, t0 + 1)
                nc.vector.tensor_reduce(nmax[:, :], lg[:, 0:EXP], AX.X, ALU.max, negate=True)\
                    .then_inc(s_lg[0], 1)
                wait(dve, s_ex[0], s.tile(1))
                nc.vector.tensor_tensor(dif[:, :, :], ex[:, :].unsqueeze(1).broadcast_to([P, EXP, EXP]),
                                        ex[:, :].unsqueeze(2).broadcast_to([P, EXP, EXP]), ALU.subtract)\
                    .then_inc(s_dve, 1)
                if s.is_tile(0):
                    dve.wait_ge(s_const, 9)
                dve.wait_ge(s_dve, t0 + 2)
                nc.vector.tensor_tensor(gtm[:, :, :], dif[:, :, :], tie[:, :, :], ALU.is_gt).then_inc(s_dve, 1)
                dve.wait_ge(s_dve, t0 + 3)
                nc.vector.tensor_reduce(rank[:, :], gtm[:, :, :], AX.X, ALU.add).then_inc(s_dve, 1)
                dve.wait_ge(s_dve, t0 + 4)
                nc.vector.scalar_tensor_tensor(out=wsel[:, :], in0=rank[:, :], scalar=1.5, in1=ex[:, :],
                                               op0=ALU.is_lt, op1=ALU.mult, accum_out=wden[:, :])\
                    .then_inc(s_dve, 1)
                dve.wait_ge(s_dve, t0 + 5)
                nc.vector.reciprocal(winv[:, 0:1], wden[:, :]).then_inc(s_dve, 1)
                dve.wait_ge(s_dve, t0 + 6)
                weigh(0)

            def weigh(i):
                nc.vector.scalar_tensor_tensor(
                    out=hw[:, :].rearrange("p (e r) -> p e r", e=EXP),
                    in0=gat[:, 0:ER].rearrange("p (e r) -> p e r", e=EXP), scalar=winv[:, 0:1],
                    in1=wsel[:, :].unsqueeze(2).broadcast_to([P, EXP, RANK]),
                    op0=ALU.mult, op1=ALU.mult).then_inc(s_hw[i], 1)

            def gate1(s):
                t0 = s.tile() * (DEPTH0 + DEPTH1) + DEPTH0 - DEPTH1
                if not s.there(0):
                    t0 = TILES * DEPTH0 + s.tile(-1) * DEPTH1
                wait(dve, s_g[1], s.tile(0))
                nc.vector.tensor_scalar(lg[:, :], gat[:, ER:ER + EXP + 1], PSUM1, None, ALU.mult)\
                    .then_inc(s_dve, 1)
                dve.wait_ge(s_dve, t0 + 1)
                nc.vector.tensor_reduce(nmax[:, :], lg[:, 0:EXP], AX.X, ALU.max, negate=True)\
                    .then_inc(s_lg[1], 1)
                wait(dve, s_ex[1], s.tile(0) * 2)
                nc.vector.tensor_scalar(wsum[:, 1:2], wsum[:, 1:2], 1.0, None, ALU.add).then_inc(s_dve, 1)
                dve.wait_ge(s_dve, t0 + 2)
                nc.vector.reciprocal(winv[:, :], wsum[:, :]).then_inc(s_dve, 1)
                dve.wait_ge(s_dve, t0 + 3)
                nc.vector.tensor_scalar(thr[:, :], winv[:, 1:2], MAX_THR, None, ALU.mult).then_inc(s_dve, 1)
                dve.wait_ge(s_dve, t0 + 4)
                nc.vector.tensor_scalar(rank[:, :], ex[:, :], winv[:, 0:1], thr[:, 0:1], ALU.mult,
                                        ALU.subtract).then_inc(s_dve, 1)
                dve.wait_ge(s_dve, t0 + 5)
                nc.vector.tensor_scalar(wsel[:, :], rank[:, :], 0.0, None, ALU.max).then_inc(s_dve, 1)
                dve.wait_ge(s_dve, t0 + 6)
                nc.vector.tensor_reduce(wden[:, :], wsel[:, :], AX.X, ALU.add).then_inc(s_dve, 1)
                dve.wait_ge(s_dve, t0 + 7)
                nc.vector.scalar_tensor_tensor(out=thr[:, :], in0=wden[:, :], scalar=0.0, in1=wden[:, :],
                                               op0=ALU.is_equal, op1=ALU.add).then_inc(s_dve, 1)
                dve.wait_ge(s_dve, t0 + 8)
                nc.vector.reciprocal(winv[:, 0:1], thr[:, :]).then_inc(s_dve, 1)
                dve.wait_ge(s_dve, t0 + 9)
                weigh(1)

            def body(s):
                if s.there(-1):
                    wait(dve, s_z, s.tile(0))
                    if s.there(0):
                        wait(dve, s_yl, s.tile(1))
                    nc.vector.scalar_tensor_tensor(
                        out=act32[:, :, :], in0=mix[:, :].rearrange("p (j n) -> p j n", n=D),
                        scalar=1.0 / S_AGG,
                        in1=row_of(aggb, s.tile(-1)).unsqueeze(1).broadcast_to([P, KT, D]),
                        op0=ALU.mult, op1=ALU.add).then_inc(s_z32, 1)
                if s.there(-2):
                    wait(dve, s_acc[1], s.tile(-1))
                    wait(dve, s_x1b, s.tile(-1))
                    if s.is_tile(2) or s.is_tile(3):
                        dve.wait_ge(s_split_l, 2 * LAYER0)
                    if s.there(-4):
                        wait(dve, s_out[s.slot()], s.pair(-2) * 16)
                    nc.vector.scalar_tensor_tensor(out=stage[:, s.slot(), 0:L], in0=acc[1][:, :], scalar=PSUM1,
                                                   in1=x1[:, s.slot(), :], op0=ALU.mult, op1=ALU.add)\
                        .then_inc(s_o, 1)
                if s.there(0):
                    gate0(s)
                if s.is_tile(0):
                    for n in range(LAYER0, LAYER0 + 4):
                        split_low(n)
                if s.there(-1):
                    wait(dve, s_zh, s.tile(0))
                    nc.vector.tensor_tensor(zl[:, :, :], act32[:, :, :], zh[:, :, :], ALU.subtract)\
                        .then_inc(s_zl, 1)
                if s.there(2):
                    split_x(s)
                if s.is_tile(-2):
                    prelude()
                if s.there(0):
                    wait(dve, s_hth[0], s.tile(1))
                    low(hwl[:, :], hwt[:, 0:D], hwh[:, :], S_HW, s_htl[0])
                if s.there(1):
                    wait(dve, s_conv, s.tile(2))
                    wait(dve, s_zl, s.tile(0))
                    nc.vector.tensor_tensor(
                        y_out, conv_out,
                        row_of(ctxb, s.tile(1)).rearrange("p (g o) -> p g o", g=NNG).unsqueeze(2)
                        .broadcast_to([P, NNG, PH, CG]), ALU.add).then_inc(s_y32, 1)
                    wait(dve, s_yh, s.tile(2))
                    nc.vector.tensor_tensor(yl[:, :, :], act32[:, :, :], yh[:, :, :], ALU.subtract)\
                        .then_inc(s_yl, 1)
                if s.is_tile(0, 1):
                    for n in range(LAYER0):
                        split_low(n)
                if s.there(0):
                    wait(dve, s_acc[0], s.tile(1))
                    wait(dve, s_xb, s.tile(1))
                    wait(dve, s_o, s.tile(-1))
                    if s.is_tile(0):
                        dve.wait_ge(s_toep_l, 1)
                    if s.is_tile(1):
                        dve.wait_ge(s_rowsum, 16)
                    nc.vector.scalar_tensor_tensor(out=x1[:, s.slot(), :], in0=acc[0][:, :], scalar=PSUM0,
                                                   in1=xb[:, s.slot(), :], op0=ALU.mult, op1=ALU.add)\
                        .then_inc(s_x1, 1)
                    wait(dve, s_aggh, s.tile(1))
                    for h in range(2):
                        a = nc.vector.scalar_tensor_tensor(
                            out=aggl[h * CH:(h + 1) * CH, h * CH:(h + 1) * CH], in0=agg_of(h, s.tile()),
                            scalar=S_AGG, in1=aggh[h * CH:(h + 1) * CH, h * CH:(h + 1) * CH],
                            op0=ALU.mult, op1=ALU.subtract)
                    a.then_inc(s_aggl, 1)
                    wait(dve, s_x1h, s.tile(1))
                    nc.vector.tensor_tensor(x1l[:, :], x1[:, s.slot(), :], x1h[:, :], ALU.subtract)\
                        .then_inc(s_x1l, 1)
                if s.is_tile(0):
                    for n in range(LAYER0 + 4, 2 * LAYER0):
                        split_low(n)
                if s.there(-1):
                    gate1(s)
                    wait(dve, s_hth[1], s.tile(0))
                    low(hwl[:, :], hwt[:, 0:D], hwh[:, :], S_HW, s_htl[1])

            pipeline(dve, body, TILES // 2 - 1, (-1, 4))

        @block.tensor
        def _(pe):
            def gates(i, ah, al, wh, wl, width, k, first, last):
                for n, (a, w) in enumerate(((ah, wh), (ah, wl), (al, wh))):
                    m = nc.tensor.matmul(gat[:, 0:width], a[:, k, :], w[:, k, L:L + width],
                                         start=(first and n == 0), stop=(last and n == 2))
                return m

            def base(i, ah, al, wh, wl, k):
                for n, (a, w) in enumerate(((ah, wh), (ah, wl), (al, wh))):
                    for h in range(2):
                        nc.tensor.matmul(acc[i][:, h * HALF:(h + 1) * HALF], a[:, k, :],
                                         w[:, k, h * HALF:(h + 1) * HALF],
                                         start=(k == 0 and n == 0), stop=False)

            def lora_b(i):
                for n, (a, w) in enumerate(((hwh, bh[i]), (hwh, bl[i]), (hwl, bh[i]))):
                    for h in range(2):
                        m = nc.tensor.matmul(acc[i][:, h * HALF:(h + 1) * HALF], a[:, :],
                                             w[:, h * HALF:(h + 1) * HALF], start=False, stop=(n == 2))
                m.then_inc(s_acc[i], 1)

            def turn_hw(i):
                nc.tensor.transpose(hwt[:, 0:D], hw[:, :], ident[:, :]).then_inc(s_ht[i], 1)

            def conv(s):
                for g in range(NNG):
                    c0 = (g % NGRP) * CG
                    for n, (part, band) in enumerate(((0, toep_h), (0, toep_l), (1, toep_h))):
                        for b in range(2):
                            m = nc.tensor.matmul(mix[:, g * P:(g + 1) * P],
                                                 xp[:, s.slot(1), g, part, b:b + P],
                                                 band[:, PH * b:PH * (b + 1), c0:c0 + CG],
                                                 start=(n == 0 and b == 0), stop=(n == 2 and b == 1))
                m.then_inc(s_conv, 1)

            def mixing():
                for j in range(KT):
                    for n, (a, w) in enumerate(((x1h, aggh), (x1h, aggl), (x1l, aggh))):
                        m = nc.tensor.matmul(mix[:, j * D:(j + 1) * D], a[:, j * P:(j + 1) * P], w[:, :],
                                             start=(n == 0), stop=(n == 2))
                m.then_inc(s_z, 1)

            def row_sums(n):
                pe.wait_ge(s_prod, n + 1)
                if n >= 4:
                    pe.wait_ge(s_rowout, n - 3)
                rows_ = CD if n < 8 else NK
                nc.tensor.matmul(bank[n % 4], ones[0:rows_, :],
                                 prod[0:rows_, n % 2, :, :].rearrange("p b o -> p (b o)"),
                                 start=True, stop=True).then_inc(s_rowsum, 1)

            def prelude():
                pe.wait_ge(s_const, 3)
                for n in range(8):
                    row_sums(n)
                pe.wait_ge(s_cond, 16 * 3)
                pe.wait_ge(s_mlp, 16 * 9)
                nc.tensor.matmul(hwt[:, 0:NB], mw0[:, :], embt[:, :], start=True, stop=True).then_inc(s_mlp_mm, 1)
                pe.wait_ge(s_mlp_act, 1)
                nc.tensor.matmul(gat[:, 0:NB], mw1[:, :], h1[:, :], start=True, stop=True).then_inc(s_mlp_mm, 1)
                pe.wait_ge(s_mlp_act, 2)
                nc.tensor.matmul(hwt[0:NB, 256:256 + NK], h2[:, :], mw2[:, :], start=True, stop=True)\
                    .then_inc(s_mlp_mm, 1)

            def prelude_agg():
                pe.wait_ge(s_mlp_dve, 4)
                pe.wait_ge(s_const, 9)
                nc.tensor.transpose(gat[0:NK, 256:256 + NB], att[:, :], ident[0:NB, 0:NB]).then_inc(s_attt, 1)
                for n in range(8, 16):
                    row_sums(n)
                for q in range(2):
                    for h in range(2):
                        if q == 0:
                            pe.wait_ge(s_rowout, 16)
                        else:
                            pe.wait_ge(s_agg_out, h + 1)
                        for o in range(16):
                            m = nc.tensor.matmul(
                                acc[h][:, o * NB:(o + 1) * NB],
                                kw[:, 32 * q + 16 * h + o, :, :].rearrange("k a i -> k (a i)"),
                                attt[:, :], start=True, stop=True)
                        m.then_inc(s_agg, 1)

            def body(s):
                if s.is_tile(-1):
                    prelude()
                if s.there(0):
                    wait(pe, s_yh, s.tile(1))
                    wait(pe, s_yl, s.tile(1))
                    if s.is_tile(0):
                        pe.wait_ge(s_agg_out, 4)
                        for k in range(KT):
                            pe.wait_ge(s_split_h, k + 1)
                            pe.wait_ge(s_split_l, k + 1)
                            m = gates(0, yh, yl, w0h, w0l, G0W, k, k == 0, k == KT - 1)
                            base(0, yh, yl, w0h, w0l, k)
                        m.then_inc(s_g[0], 1)
                        pe.wait_ge(s_split_l, LAYER0)
                    else:
                        for k in range(KT):
                            m = gates(0, yh, yl, w0h, w0l, G0W, k, k == 0, k == KT - 1)
                        m.then_inc(s_g[0], 1)
                        for k in range(KT):
                            base(0, yh, yl, w0h, w0l, k)
                    wait(pe, s_hw[0], s.tile(1))
                    turn_hw(0)
                if s.there(1):
                    if s.is_tile(0, 1):
                        pe.wait_ge(s_toep_l, 1)
                    wait(pe, s_xp[s.slot(1)], (s.pair(1) + 1) * 16 * NNG)
                    wait(pe, s_z32, s.tile(0))
                    conv(s)
                if s.is_tile(-1):
                    prelude_agg()
                if s.there(0):
                    wait(pe, s_hth[0], s.tile(1))
                    wait(pe, s_htl[0], s.tile(1))
                    lora_b(0)
                if s.there(-1):
                    wait(pe, s_zh, s.tile(0))
                    wait(pe, s_zl, s.tile(0))
                    if s.is_tile(0, -1):
                        pe.wait_ge(s_split_l, 2 * LAYER0)
                    wait(pe, s_o, s.tile(-1))
                    for k in range(KT):
                        m = gates(1, zh, zl, w1h, w1l, G1W, k, k == 0, k == KT - 1)
                    m.then_inc(s_g[1], 1)
                    for k in range(KT):
                        base(1, zh, zl, w1h, w1l, k)
                    wait(pe, s_hw[1], s.tile(0))
                    turn_hw(1)
                if s.there(0):
                    wait(pe, s_x1h, s.tile(1))
                    wait(pe, s_x1l, s.tile(1))
                    wait(pe, s_aggl, s.tile(1))
                    if s.there(1):
                        wait(pe, s_y32, s.tile(2))
                    mixing()
                if s.there(-1):
                    wait(pe, s_hth[1], s.tile(0))
                    wait(pe, s_htl[1], s.tile(0))
                    lora_b(1)

            pipeline(pe, body, TILES // 2 - 1, (-1, 3))


def kernel(**inputs):
    import numpy as _np
    import concourse.bacc as _bacc
    from concourse import mybir as _mybir
    from concourse.bass_utils import run_bass_kernel_spmd as _run

    a = {k: _np.asarray(v) for k, v in inputs.items()}
    w0 = _np.concatenate([a["L0_ffn_W_base"], a["L0_ffn_lora_A"].reshape(ER, L), a["L0_ffn_W_router"]])
    w1 = _np.concatenate([a["L1_ffn_W_base"], a["L1_ffn_A_w"].reshape(ER, L), a["L1_ffn_W_gate"],
                          a["L1_ffn_W_thr"].reshape(1, L)])
    args = [
        ("x", a["x"].reshape(NB * CH, L)),
        ("emb_t", a["cond_128"].T),
        ("fside", a["fside_S_0"]),
        ("conv_w", a["L0_cond_weight"].transpose(1, 2, 0)),
        ("cw_t", a["L0_cond_c_weight"].T),
        ("w_l0", w0.reshape(L + G0W, P, PH)[:, :, ::-1].transpose(1, 2, 0)),
        ("lora_b0", a["L0_ffn_lora_B"].transpose(0, 2, 1).reshape(ER, L)),
        ("b_l0", a["L0_ffn_b_base"]),
        ("mlp_w0", a["L1_cond_W0"]),
        ("mlp_b0", a["L1_cond_b0"].reshape(HID, 1)),
        ("mlp_w1", a["L1_cond_W1"]),
        ("mlp_b1", a["L1_cond_b1"].reshape(HID, 1)),
        ("mlp_w2", a["L1_cond_W2"]),
        ("mlp_b2", a["L1_cond_b2"]),
        ("kern_w", a["L1_cond_weight"].reshape(NK, CH, CH)),
        ("kern_b", a["L1_cond_bias_k"]),
        ("w_l1", w1.reshape(L + G1W, KT, P).transpose(2, 1, 0)),
        ("lora_b1", a["L1_ffn_B_w"].transpose(0, 2, 1).reshape(ER, L)),
        ("b_l1", a["L1_ffn_b_base"]),
        ("b_thr", a["L1_ffn_b_thr"]),
    ]
    nc = _bacc.Bacc("TRN2", target_bir_lowering=False, num_devices=1)
    arrays, aps = {}, {}
    for name, v in args:
        v = _np.ascontiguousarray(v)
        arrays[f"{name}_dram"] = v
        aps[name] = nc.dram_tensor(f"{name}_dram", v.shape, _mybir.dt.from_np(v.dtype), kind="ExternalInput").ap()
    aps["out"] = nc.dram_tensor("out_dram", (NB * CH, L), _mybir.dt.float32, kind="ExternalOutput").ap()
    adaln_ffn(nc, **aps)
    r = _run(nc, [arrays], core_ids=[0])
    return r.results[0]["out_dram"].reshape(NB, CH, L)
```

```python
from contextlib import ExitStack

import concourse.bass as bass
from concourse import mybir

F32 = mybir.dt.float32
F16 = mybir.dt.float16
ALU = mybir.AluOpType
ACT = mybir.ActivationFunctionType
AX = mybir.AxisListType

P = 128
NB, CH, L = 64, 64, 1024
D = CH * 2
TILES = NB // 2
KT = L // P
PH = 8
NGRP, CG, TAPS = 4, 16, 9
NNG = 2 * NGRP
BLK = L // PH + 1
BLKP = BLK + 1
EXP, RANK = 8, 16
ER = EXP * RANK
CD, HID, NK = 128, 128, 8
HALF = L // 2
G0W, G1W = ER + EXP, ER + EXP + 1
WROW = 1168
STAGES = 3

S_CONV = 4.0
S_W = 1024.0
S_AGG = 64.0
S_HW = 2.0 / S_W
PSUM0 = 1.0 / (S_CONV * S_W)
PSUM1 = 1.0 / S_W
TINY = 1.1754944e-38
MAX_THR = 0.125


def wait(eng, sem, n):
    if isinstance(n, int) and n <= 0:
        return
    eng.wait_ge(sem, n)


class Step:

    def __init__(self, j, off, known=None):
        self.j, self.off, self.known = j, off, known

    def tile(self, d=0):
        return self.known[self.off + d] if self.known else self.j * 2 + self.off + d

    def pair(self, d=0):
        return self.j + (self.off + d) // 2

    def slot(self, d=0):
        return (self.off + d) % 2

    def there(self, d=0):
        return self.known is not None or 0 <= self.tile(d) < TILES

    def is_tile(self, n, d=0):
        return self.known is None and self.tile(d) == n


def pipeline(eng, body, loop_to, reach):
    for j in (-1, 0, 1):
        for off in (0, 1):
            body(Step(j, off))
    with eng.Fori(2, loop_to) as j:
        known = {n: j * 2 + n for n in range(reach[0], reach[1] + 1)}
        for count in known.values():
            eng.compute_val(count)
        for off in (0, 1):
            body(Step(j, off, known))
    for j in range(loop_to, TILES // 2 + 1):
        for off in (0, 1):
            body(Step(j, off))


def adaln_ffn(nc, x, emb_t, fside, conv_w, cw_t, w_l0, lora_b0, b_l0, mlp_w0, mlp_b0, mlp_w1,
              mlp_b1, mlp_w2, mlp_b2, kern_w, kern_b, w_l1, lora_b1, b_l1, b_thr, out):
    with ExitStack() as ctx:
        def sb(name, shape, dt=F32, stack=ctx):
            return stack.enter_context(nc.sbuf_tensor(name, shape, dt))

        def sem(name):
            return ctx.enter_context(nc.semaphore(name))

        w0 = sb("w0", [P, KT, 2, WROW], F16)
        bh = [sb(f"b{i}h", [P, L], F16) for i in range(2)]
        bl = [sb(f"b{i}l", [P, L], F16) for i in range(2)]
        toep_h = sb("toep_h", [P, 2 * PH, CH], F16)
        toep_l = sb("toep_l", [P, 2 * PH, CH], F16)
        ctxb = sb("ctxb", [P, NB * CH])
        aggb = sb("aggb", [P, NB * CH])
        agg_t = sb("agg_t", [P, TILES, CH])
        brow = [sb(f"brow{i}", [P, L]) for i in range(2)]
        ident = sb("ident", [P, P])
        sel = sb("sel", [P, NB], F16)
        tie = sb("tie", [P, EXP, EXP])
        bthr = sb("bthr", [P, 1])
        nthr = sb("nthr", [P, 1])
        x_in = sb("x_in", [P, 2, L])
        xb = sb("xb", [P, 2, L])
        xs = sb("xs", [P, 2, PH, 2, BLKP], F16)
        xp = sb("xp", [P, 2, NNG, 2, BLKP], F16)
        act32 = sb("act32", [P, KT, D])
        yh = sb("yh", [P, KT, D], F16)
        yl = sb("yl", [P, KT, D], F16)
        zh = sb("zh", [P, KT, D], F16)
        zl = sb("zl", [P, KT, D], F16)
        x1 = sb("x1", [P, 2, L])
        x1h = sb("x1h", [P, L], F16)
        x1l = sb("x1l", [P, L], F16)
        aggh = sb("aggh", [P, D], F16)
        aggl = sb("aggl", [P, D], F16)
        stage = sb("stage", [P, STAGES, WROW])
        lg = sb("lg", [P, EXP + 1])
        nmax = sb("nmax", [P, 1])
        ex = sb("ex", [P, EXP])
        dif = sb("dif", [P, EXP, EXP])
        gtm = sb("gtm", [P, EXP, EXP])
        rank = sb("rank", [P, EXP])
        wsel = sb("wsel", [P, EXP])
        wsum = sb("wsum", [P, 2])
        wden = sb("wden", [P, 1])
        winv = sb("winv", [P, 2])
        thr = sb("thr", [P, 1])
        hw = sb("hw", [P, ER])
        hwh = sb("hwh", [P, D], F16)
        hwl = sb("hwl", [P, D], F16)

        with ExitStack() as pre:
            kw = sb("kw", [NK, CH, CH], F32, pre)
            kb = sb("kb", [NK, CH], F32, pre)
            embt = sb("embt", [CD, NB], F32, pre)
            cwt = sb("cwt", [CD, CH], F32, pre)
            fsb = sb("fsb", [NB, CH], F32, pre)
            row32 = sb("row32", [NB, 2, CH], F32, pre)
            row16 = sb("row16", [P, 2, CH], F16, pre)
            mw0 = sb("mw0", [CD, HID], F32, pre)
            mw1 = sb("mw1", [HID, HID], F32, pre)
            mw2 = sb("mw2", [HID, NK], F32, pre)
            mb0 = sb("mb0", [HID, 1], F32, pre)
            mb1 = sb("mb1", [HID, 1], F32, pre)
            mb2 = sb("mb2", [NB, NK], F32, pre)
            h1 = sb("h1", [HID, NB], F32, pre)
            h2 = sb("h2", [HID, NB], F32, pre)
            alg = sb("alg", [NB, NK], F32, pre)
            anm = sb("anm", [NB, 1], F32, pre)
            aex = sb("aex", [NB, NK], F32, pre)
            asum = sb("asum", [NB, 1], F32, pre)
            ainv = sb("ainv", [NB, 1], F32, pre)
            att = sb("att", [NB, NK], F32, pre)
            attt = sb("attt", [NK, NB], F32, pre)
        w1 = sb("w1", [P, KT, 2, WROW], F16)
        toep = x1[:, 0, :].rearrange("p (c o) -> p c o", o=CH)

        acc = [ctx.enter_context(nc.psum_tensor(f"acc{i}", [P, L], F32)) for i in range(2)]
        mix = ctx.enter_context(nc.psum_tensor("mix", [P, L], F32))
        gat = ctx.enter_context(nc.psum_tensor("gat", [P, HALF], F32))
        hwt = ctx.enter_context(nc.psum_tensor("hwt", [P, HALF], F32))

        s_zero = sem("s_zero")
        s_const = sem("s_const")
        s_toep = sem("s_toep")
        s_cond = sem("s_cond")
        s_mlp = sem("s_mlp")
        s_kern = sem("s_kern")
        s_rows = sem("s_rows")
        s_nthr = sem("s_nthr")
        s_toep_h = sem("s_toep_h")
        s_toep_l = sem("s_toep_l")
        s_row_mm = sem("s_row_mm")
        s_row = sem("s_row")
        s_bcast = sem("s_bcast")
        s_bcast_out = sem("s_bcast_out")
        s_mlp_mm = sem("s_mlp_mm")
        s_mlp_act = sem("s_mlp_act")
        s_mlp_dve = sem("s_mlp_dve")
        s_agg = sem("s_agg")
        s_agg_out = sem("s_agg_out")
        s_stage = [sem(f"s_stage{i}") for i in range(STAGES)]
        s_split_h = sem("s_split_h")
        s_split_l = sem("s_split_l")
        s_x = [sem(f"s_xin{i}") for i in range(2)]
        s_xh = sem("s_xh")
        s_xl = sem("s_xl")
        s_xp = [sem(f"s_xp{i}") for i in range(2)]
        s_xb = sem("s_xb")
        s_conv = sem("s_conv")
        s_y32 = sem("s_y32")
        s_yh = sem("s_yh")
        s_yl = sem("s_yl")
        s_g = [sem("s_g0"), sem("s_g1")]
        s_lg = [sem("s_lg0"), sem("s_lg1")]
        s_ex = [sem("s_ex0"), sem("s_ex1")]
        s_dve = sem("s_dve")
        s_hw = [sem("s_hw0"), sem("s_hw1")]
        s_ht = [sem("s_ht0"), sem("s_ht1")]
        s_hth = [sem("s_hth0"), sem("s_hth1")]
        s_htl = [sem("s_htl0"), sem("s_htl1")]
        s_acc = [sem("s_acc0"), sem("s_acc1")]
        s_x1 = sem("s_x1")
        s_x1h = sem("s_x1h")
        s_x1l = sem("s_x1l")
        s_x1b = sem("s_x1b")
        s_aggh = sem("s_aggh")
        s_aggl = sem("s_aggl")
        s_z = sem("s_z")
        s_z32 = sem("s_z32")
        s_zh = sem("s_zh")
        s_zl = sem("s_zl")
        s_o = sem("s_o")
        s_out = [sem(f"s_out{i}") for i in range(2)]

        def weights(src, dst, width):
            return [(src[:, k, :], dst[:, k, 0, 0:width], dst[:, k, 1, 0:width], width) for k in range(KT)]

        lora = [(b, bh[i][:, :], bl[i][:, :], L) for i, b in enumerate((lora_b0, lora_b1))]
        first, second = weights(w_l0, w0, L + G0W), weights(w_l1, w1, L + G1W)
        pieces = first + lora[:1] + second[5:] + lora[1:] + second[:5]
        LAYER0 = KT + 1
        CLEAR = LAYER0 + 4

        def by_phase(slot):
            v = x_in[:, slot, :].rearrange("p (b f) -> p f b", f=PH)
            return ((v[:, PH // 2:PH, :], 0, PH // 2, 1), (v[:, 0:PH // 2, :], PH // 2, PH, 0))

        def bcast_acc(n):
            return acc[n % 2 if n < 4 else 1]

        conv_out = mix[:, :].rearrange("p (g c o) -> p g c o", g=NNG, c=PH)
        y_out = act32[:, :, :].rearrange("p c (g o) -> p g c o", g=NNG)

        def row_of(tab, n):
            return tab[:, bass.ds(n * D, D)] if not isinstance(n, int) else tab[:, n * D:(n + 1) * D]

        def agg_of(h, n):
            part = agg_t[h * CH:(h + 1) * CH, bass.ds(n, 1), :] if not isinstance(n, int) else \
                agg_t[h * CH:(h + 1) * CH, n:n + 1, :]
            return part.rearrange("p a o -> p (a o)")

        def rows(ap, n):
            return ap[bass.ds(n * D, D), :] if not isinstance(n, int) else ap[n * D:(n + 1) * D, :]

        block = ctx.enter_context(nc.Block())

        @block.sync
        def _(sp):
            def load_x(slot, n):
                sp.dma_start(x_in[:, slot, :], rows(x, n)).then_inc(s_x[slot], 16)

            def put_stage(n):
                sp.wait_ge(s_split_h, n - STAGES + 1)
                sp.wait_ge(s_split_l, n - STAGES + 1)
                src, _, _, width = pieces[n]
                sp.dma_start(stage[:, n % STAGES, 0:width], src).then_inc(s_stage[n % STAGES], 16)

            load_x(0, 0)
            for dst, src in ((embt, emb_t), (cwt, cw_t)):
                sp.dma_start(dst[:, :], src).then_inc(s_cond, 16)
            sp.dma_start(fsb[:, :], fside.partition_broadcast(NB)).then_inc(s_cond, 16)
            sp.wait_ge(s_zero, 1)
            for f in range(PH):
                sp.dma_start(toep[f:P:PH, PH - 1 - f:PH - 1 - f + TAPS, :], conv_w).then_inc(s_toep, 16)
            load_x(1, 1)

            def body(s):
                if s.there(-2):
                    wait(sp, s_o, s.tile(-1))
                if s.there(3) and not s.is_tile(1, 3):
                    wait(sp, s_xb, s.tile(2))
                if s.there(2):
                    wait(sp, s_xh, s.tile(3))
                    wait(sp, s_xl, s.tile(3))
                    wait(sp, s_conv, s.tile(1))
                    for g in range(NNG):
                        sp.dma_start(xp[:, s.slot(), g, :, :].rearrange("p h b -> p (h b)"),
                                     xs[g * CG:(g + 1) * CG, s.slot(), :, :, :]
                                     .rearrange("i f h b -> i f (h b)")).then_inc(s_xp[s.slot()], 16)
                if s.is_tile(-2):
                    for n in range(STAGES, LAYER0):
                        put_stage(n)
                if s.is_tile(-1):
                    for n in range(LAYER0, LAYER0 + 3):
                        put_stage(n)
                if s.is_tile(0):
                    for n in range(LAYER0 + 3, len(pieces)):
                        put_stage(n)
                if s.there(-2):
                    sp.dma_start(rows(out, s.tile(-2)), stage[:, s.slot(), 0:L]).then_inc(s_out[s.slot()], 16)
                if s.there(3) and not s.is_tile(1, 3):
                    load_x(s.slot(3), s.tile(3))

            pipeline(sp, body, TILES // 2 - 2, (-2, 4))
            for p in range(2):
                sp.wait_ge(s_out[p], 16 * TILES // 2)

        @block.gpsimd
        def _(pool):
            for dst, src in ((mw0[:, :], mlp_w0), (mb0[:, :], mlp_b0), (mw1[:, :], mlp_w1),
                             (mb1[:, :], mlp_b1), (mw2[:, :], mlp_w2),
                             (mb2[:, :], mlp_b2.partition_broadcast(NB))):
                pool.dma_start(dst, src).then_inc(s_mlp, 16)
            nc.gpsimd.memset(sel[:, :], 0.0).then_inc(s_const, 1)
            nc.gpsimd.memset(ident[:, :], 0.0).then_inc(s_const, 1)
            pool.wait_ge(s_const, 2)
            for h in range(2):
                nc.gpsimd.affine_select(out=sel[:, :], in_=sel[:, :], compare_op=ALU.not_equal, fill=1.0,
                                        base=-h * NB, pattern=[[-1, NB]], channel_multiplier=1)\
                    .then_inc(s_const, 1)
                pool.wait_ge(s_const, 3 + h)
            nc.gpsimd.affine_select(out=ident[:, :], in_=ident[:, :], compare_op=ALU.not_equal, fill=1.0,
                                    base=0, pattern=[[-1, P]], channel_multiplier=1).then_inc(s_const, 1)
            for dst, src in ((kb[:, :], kern_b), (kw[:, :, :], kern_w)):
                pool.dma_start(dst, src).then_inc(s_kern, 16)
            for dst, src in ((bthr, b_thr), (brow[0], b_l0), (brow[1], b_l1)):
                pool.dma_start(dst[:, :], src.partition_broadcast(P)).then_inc(s_rows, 16)
            nc.gpsimd.memset(tie[:, :, :], 0.0).then_inc(s_const, 1)
            nc.gpsimd.memset(aggh[:, :], 0.0).then_inc(s_const, 1)
            nc.gpsimd.memset(aggl[:, :], 0.0).then_inc(s_const, 1)
            pool.wait_ge(s_const, 6)
            nc.gpsimd.affine_select(out=tie[:, :, :], in_=tie[:, :, :], compare_op=ALU.is_ge, fill=-TINY,
                                    base=0, pattern=[[-1, EXP], [1, EXP]], channel_multiplier=0)\
                .then_inc(s_const, 1)

            def body(s):
                if s.there(0):
                    wait(pool, s_x1, s.tile(1))
                    wait(pool, s_x1h, s.tile(1))
                    wait(pool, s_x1l, s.tile(1))
                    if s.is_tile(0):
                        pool.wait_ge(s_rows, 16 * 3)
                    nc.gpsimd.tensor_tensor(x1[:, s.slot(), :], x1[:, s.slot(), :], brow[1][:, :], ALU.add)\
                        .then_inc(s_x1b, 1)
                if s.there(2):
                    wait(pool, s_x[s.slot()], (s.pair(2) + 1) * 16)
                    wait(pool, s_x1, s.tile(1))
                    if s.is_tile(0, 2):
                        pool.wait_ge(s_rows, 16 * 3)
                    nc.gpsimd.tensor_tensor(xb[:, s.slot(), :], x_in[:, s.slot(), :], brow[0][:, :], ALU.add)\
                        .then_inc(s_xb, 1)

            pipeline(pool, body, TILES // 2 - 1, (1, 4))

        @block.scalar
        def _(act):
            def split_high(n):
                if n == CLEAR:
                    act.wait_ge(s_agg, 2)
                _, dst, _, width = pieces[n]
                act.wait_ge(s_stage[n % STAGES], 16 * (n // STAGES + 1))
                nc.scalar.activation(dst, stage[:, n % STAGES, 0:width], ACT.Copy, scale=S_W).then_inc(s_split_h, 1)

            def rows_out(n):
                act.wait_ge(s_bcast, n + 1)
                k = n % 4
                nc.scalar.activation((ctxb, aggb)[n // 4][:, k * L:(k + 1) * L], bcast_acc(n)[:, :], ACT.Copy)\
                    .then_inc(s_bcast_out, 1)

            def agg_out(r):
                act.wait_ge(s_agg, r + 1)
                for q in range(2):
                    for e in range(2):
                        src = acc[1][q * CH:(q + 1) * CH, :].rearrange("p (o b) -> p b o", b=NB)
                        a = nc.scalar.activation(agg_t[e * CH:(e + 1) * CH, :, 32 * r + q:32 * r + 32:2],
                                                 src[:, e:NB:2, :], ACT.Copy)
                a.then_inc(s_agg_out, 1)

            for n in range(STAGES):
                act.dma_start(stage[:, n, 0:pieces[n][3]], pieces[n][0]).then_inc(s_stage[n], 16)

            def split_x(s):
                wait(act, s_x[s.slot()], (s.pair(2) + 1) * 16)
                if s.there(0):
                    wait(act, s_xp[s.slot()], (s.pair() + 1) * 16 * NNG)
                for n, (src, f0, f1, b0) in enumerate(by_phase(s.slot())):
                    a = nc.scalar.activation(xs[:, s.slot(), f0:f1, 0, b0:b0 + BLK - 1], src, ACT.Copy)
                a.then_inc(s_xh, 1)

            def prelude():
                act.wait_ge(s_mlp, 16 * 6)
                act.wait_ge(s_mlp_mm, 1)
                nc.scalar.activation(h1[:, :], hwt[:, 0:NB], ACT.Gelu, bias=mb0[:, 0:1]).then_inc(s_mlp_act, 1)
                act.wait_ge(s_toep, 16 * PH)
                nc.scalar.activation(toep_h[:, :, :], toep[:, :, :], ACT.Copy, scale=S_CONV).then_inc(s_toep_h, 1)
                act.wait_ge(s_mlp_mm, 2)
                nc.scalar.activation(h2[:, :], gat[:, 0:NB], ACT.Gelu, bias=mb1[:, 0:1]).then_inc(s_mlp_act, 1)
                rows_out(0)
                split_high(0)
                act.wait_ge(s_mlp_dve, 2)
                nc.scalar.activation(aex[:, :], alg[:, :], ACT.Exp, bias=anm[:, 0:1], accum_out=asum[:, 0:1])\
                    .then_inc(s_mlp_act, 1)
                rows_out(1)
                split_high(1)
                rows_out(2)
                split_high(2)
                rows_out(3)

            def body(s):
                if s.there(-1):
                    wait(act, s_z32, s.tile(0))
                    nc.scalar.activation(zh[:, :, :], act32[:, :, :], ACT.Copy).then_inc(s_zh, 1)
                if s.there(0):
                    wait(act, s_lg[0], s.tile(1))
                    nc.scalar.activation(ex[:, :], lg[:, 0:EXP], ACT.Exp, bias=nmax[:, 0:1])\
                        .then_inc(s_ex[0], 1)
                if s.there(2) and not s.is_tile(1, 2):
                    if s.is_tile(0, 2):
                        act.wait_ge(s_zero, 3)
                    split_x(s)
                if s.is_tile(-2):
                    prelude()
                if s.there(0):
                    wait(act, s_ht[0], s.tile(1))
                    nc.scalar.activation(hwh[:, :], hwt[:, 0:D], ACT.Copy, scale=S_HW).then_inc(s_hth[0], 1)
                if s.there(1):
                    wait(act, s_y32, s.tile(2))
                    nc.scalar.activation(yh[:, :, :], act32[:, :, :], ACT.Copy).then_inc(s_yh, 1)
                if s.is_tile(-1):
                    for n in range(3, LAYER0):
                        split_high(n)
                        if n == 5:
                            split_x(s)
                        if n >= 5:
                            rows_out(n - 1)
                    agg_out(0)
                    for n in range(LAYER0, LAYER0 + 3):
                        split_high(n)
                        if n == LAYER0:
                            agg_out(1)
                if s.there(0):
                    if s.is_tile(0):
                        act.wait_ge(s_agg_out, 2)
                        act.wait_ge(s_const, 8)
                    else:
                        wait(act, s_z, s.tile(0))
                    for h in range(2):
                        a = nc.scalar.activation(aggh[h * CH:(h + 1) * CH, h * CH:(h + 1) * CH],
                                                 agg_of(h, s.tile()), ACT.Copy, scale=S_AGG)
                    a.then_inc(s_aggh, 1)
                    wait(act, s_x1, s.tile(1))
                    nc.scalar.activation(x1h[:, :], x1[:, s.slot(), :], ACT.Copy).then_inc(s_x1h, 1)
                if s.is_tile(0):
                    for n in range(LAYER0 + 3, 2 * LAYER0):
                        split_high(n)
                if s.there(-1):
                    wait(act, s_lg[1], s.tile(0))
                    nc.scalar.activation(ex[:, :], lg[:, 0:EXP], ACT.Exp, bias=nmax[:, 0:1],
                                         accum_out=wsum[:, 0:1]).then_inc(s_ex[1], 1)
                    nc.scalar.activation(wsum[:, 1:2], lg[:, EXP:EXP + 1], ACT.Exp, scale=-1.0,
                                         bias=nthr[:, 0:1]).then_inc(s_ex[1], 1)
                    wait(act, s_ht[1], s.tile(0))
                    nc.scalar.activation(hwh[:, :], hwt[:, 0:D], ACT.Copy, scale=S_HW).then_inc(s_hth[1], 1)

            pipeline(act, body, TILES // 2 - 1, (-1, 4))

        @block.vector
        def _(dve):
            def low(dst, full, high, scale, done):
                return nc.vector.scalar_tensor_tensor(out=dst, in0=full, scalar=scale, in1=high,
                                                      op0=ALU.mult, op1=ALU.subtract).then_inc(done, 1)

            def split_low(n):
                _, high, dst, width = pieces[n]
                dve.wait_ge(s_split_h, n + 1)
                low(dst, stage[:, n % STAGES, 0:width], high, S_W, s_split_l)

            def split_rows(n):
                dve.wait_ge(s_row_mm, n + 1)
                scale = (S_CONV, 1.0)[n]
                if n == 0:
                    dve.wait_ge(s_cond, 16 * 3)
                    nc.vector.tensor_tensor(row32[:, n, :], gat[0:NB, 128:128 + CH], fsb[:, :], ALU.add)\
                        .then_inc(s_row, 1)
                else:
                    nc.vector.tensor_copy(row32[:, n, :], gat[0:NB, 128:128 + CH]).then_inc(s_row, 1)
                dve.wait_ge(s_row, 3 * n + 1)
                nc.vector.tensor_scalar(row16[0:NB, n, :], row32[:, n, :], scale, None, ALU.mult)\
                    .then_inc(s_row, 1)
                dve.wait_ge(s_row, 3 * n + 2)
                low(row16[NB:P, n, :], row32[:, n, :], row16[0:NB, n, :], scale, s_row)

            def prelude():
                split_rows(0)
                dve.wait_ge(s_toep_h, 1)
                low(toep_l[:, :, :], toep[:, :, :], toep_h[:, :, :], S_CONV, s_toep_l)
                dve.wait_ge(s_mlp_mm, 3)
                nc.vector.tensor_tensor(alg[:, :], hwt[0:NB, 256:256 + NK], mb2[:, :], ALU.add)\
                    .then_inc(s_mlp_dve, 1)
                dve.wait_ge(s_mlp_dve, 1)
                nc.vector.tensor_reduce(anm[:, :], alg[:, :], AX.X, ALU.max, negate=True).then_inc(s_mlp_dve, 1)
                split_low(0)
                dve.wait_ge(s_mlp_act, 3)
                nc.vector.reciprocal(ainv[:, :], asum[:, :]).then_inc(s_mlp_dve, 1)
                dve.wait_ge(s_mlp_dve, 3)
                nc.vector.tensor_scalar(att[:, :], aex[:, :], ainv[:, 0:1], None, ALU.mult).then_inc(s_mlp_dve, 1)
                split_low(1)
                dve.wait_ge(s_mlp_mm, 4)
                nc.vector.tensor_copy(attt[:, :], gat[0:NK, 256:256 + NB]).then_inc(s_mlp_dve, 1)
                split_rows(1)
                split_low(2)
                dve.wait_ge(s_rows, 16 * 3)
                nc.vector.tensor_scalar(nthr[:, :], bthr[:, :], -1.0, None, ALU.mult).then_inc(s_nthr, 1)

            def split_x(s):
                wait(dve, s_xh, s.tile(3))
                for src, f0, f1, b0 in by_phase(s.slot()):
                    a = nc.vector.tensor_tensor(xs[:, s.slot(), f0:f1, 1, b0:b0 + BLK - 1], src,
                                                xs[:, s.slot(), f0:f1, 0, b0:b0 + BLK - 1], ALU.subtract)
                a.then_inc(s_xl, 1)

            DEPTH0, DEPTH1 = 6, 9

            def gate0(s):
                t0 = s.tile() * (DEPTH0 + DEPTH1) - DEPTH1
                if s.is_tile(0):
                    t0 = 0
                wait(dve, s_g[0], s.tile(1))
                nc.vector.tensor_scalar(lg[:, 0:EXP], gat[:, ER:ER + EXP], PSUM0, None, ALU.mult)\
                    .then_inc(s_dve, 1)
                dve.wait_ge(s_dve, t0 + 1)
                nc.vector.tensor_reduce(nmax[:, :], lg[:, 0:EXP], AX.X, ALU.max, negate=True)\
                    .then_inc(s_lg[0], 1)
                wait(dve, s_ex[0], s.tile(1))
                nc.vector.tensor_tensor(dif[:, :, :], ex[:, :].unsqueeze(1).broadcast_to([P, EXP, EXP]),
                                        ex[:, :].unsqueeze(2).broadcast_to([P, EXP, EXP]), ALU.subtract)\
                    .then_inc(s_dve, 1)
                if s.is_tile(0):
                    dve.wait_ge(s_const, 9)
                dve.wait_ge(s_dve, t0 + 2)
                nc.vector.tensor_tensor(gtm[:, :, :], dif[:, :, :], tie[:, :, :], ALU.is_gt).then_inc(s_dve, 1)
                dve.wait_ge(s_dve, t0 + 3)
                nc.vector.tensor_reduce(rank[:, :], gtm[:, :, :], AX.X, ALU.add).then_inc(s_dve, 1)
                dve.wait_ge(s_dve, t0 + 4)
                nc.vector.scalar_tensor_tensor(out=wsel[:, :], in0=rank[:, :], scalar=1.5, in1=ex[:, :],
                                               op0=ALU.is_lt, op1=ALU.mult, accum_out=wden[:, :])\
                    .then_inc(s_dve, 1)
                dve.wait_ge(s_dve, t0 + 5)
                nc.vector.reciprocal(winv[:, 0:1], wden[:, :]).then_inc(s_dve, 1)
                dve.wait_ge(s_dve, t0 + 6)
                weigh(0)

            def weigh(i):
                nc.vector.scalar_tensor_tensor(
                    out=hw[:, :].rearrange("p (e r) -> p e r", e=EXP),
                    in0=gat[:, 0:ER].rearrange("p (e r) -> p e r", e=EXP), scalar=winv[:, 0:1],
                    in1=wsel[:, :].unsqueeze(2).broadcast_to([P, EXP, RANK]),
                    op0=ALU.mult, op1=ALU.mult).then_inc(s_hw[i], 1)

            def gate1(s):
                t0 = s.tile() * (DEPTH0 + DEPTH1) + DEPTH0 - DEPTH1
                if not s.there(0):
                    t0 = TILES * DEPTH0 + s.tile(-1) * DEPTH1
                wait(dve, s_g[1], s.tile(0))
                nc.vector.tensor_scalar(lg[:, :], gat[:, ER:ER + EXP + 1], PSUM1, None, ALU.mult)\
                    .then_inc(s_dve, 1)
                dve.wait_ge(s_dve, t0 + 1)
                nc.vector.tensor_reduce(nmax[:, :], lg[:, 0:EXP], AX.X, ALU.max, negate=True)\
                    .then_inc(s_lg[1], 1)
                wait(dve, s_ex[1], s.tile(0) * 2)
                nc.vector.tensor_scalar(wsum[:, 1:2], wsum[:, 1:2], 1.0, None, ALU.add).then_inc(s_dve, 1)
                dve.wait_ge(s_dve, t0 + 2)
                nc.vector.reciprocal(winv[:, :], wsum[:, :]).then_inc(s_dve, 1)
                dve.wait_ge(s_dve, t0 + 3)
                nc.vector.tensor_scalar(thr[:, :], winv[:, 1:2], MAX_THR, None, ALU.mult).then_inc(s_dve, 1)
                dve.wait_ge(s_dve, t0 + 4)
                nc.vector.tensor_scalar(rank[:, :], ex[:, :], winv[:, 0:1], thr[:, 0:1], ALU.mult,
                                        ALU.subtract).then_inc(s_dve, 1)
                dve.wait_ge(s_dve, t0 + 5)
                nc.vector.tensor_scalar(wsel[:, :], rank[:, :], 0.0, None, ALU.max).then_inc(s_dve, 1)
                dve.wait_ge(s_dve, t0 + 6)
                nc.vector.tensor_reduce(wden[:, :], wsel[:, :], AX.X, ALU.add).then_inc(s_dve, 1)
                dve.wait_ge(s_dve, t0 + 7)
                nc.vector.scalar_tensor_tensor(out=thr[:, :], in0=wden[:, :], scalar=0.0, in1=wden[:, :],
                                               op0=ALU.is_equal, op1=ALU.add).then_inc(s_dve, 1)
                dve.wait_ge(s_dve, t0 + 8)
                nc.vector.reciprocal(winv[:, 0:1], thr[:, :]).then_inc(s_dve, 1)
                dve.wait_ge(s_dve, t0 + 9)
                weigh(1)

            def body(s):
                if s.there(-1):
                    wait(dve, s_z, s.tile(0))
                    if s.there(0):
                        wait(dve, s_yl, s.tile(1))
                    nc.vector.scalar_tensor_tensor(
                        out=act32[:, :, :], in0=mix[:, :].rearrange("p (j n) -> p j n", n=D),
                        scalar=1.0 / S_AGG,
                        in1=row_of(aggb, s.tile(-1)).unsqueeze(1).broadcast_to([P, KT, D]),
                        op0=ALU.mult, op1=ALU.add).then_inc(s_z32, 1)
                if s.there(-2):
                    wait(dve, s_acc[1], s.tile(-1))
                    wait(dve, s_x1b, s.tile(-1))
                    if s.is_tile(2) or s.is_tile(3):
                        dve.wait_ge(s_split_l, 2 * LAYER0)
                    if s.there(-4):
                        wait(dve, s_out[s.slot()], s.pair(-2) * 16)
                    nc.vector.scalar_tensor_tensor(out=stage[:, s.slot(), 0:L], in0=acc[1][:, :], scalar=PSUM1,
                                                   in1=x1[:, s.slot(), :], op0=ALU.mult, op1=ALU.add)\
                        .then_inc(s_o, 1)
                if s.there(0):
                    gate0(s)
                if s.there(-1):
                    wait(dve, s_zh, s.tile(0))
                    nc.vector.tensor_tensor(zl[:, :, :], act32[:, :, :], zh[:, :, :], ALU.subtract)\
                        .then_inc(s_zl, 1)
                if s.there(2) and not s.is_tile(1, 2):
                    split_x(s)
                if s.is_tile(-2):
                    prelude()
                if s.there(0):
                    wait(dve, s_hth[0], s.tile(1))
                    low(hwl[:, :], hwt[:, 0:D], hwh[:, :], S_HW, s_htl[0])
                if s.there(1):
                    wait(dve, s_conv, s.tile(2))
                    wait(dve, s_zl, s.tile(0))
                    nc.vector.tensor_tensor(
                        y_out, conv_out,
                        row_of(ctxb, s.tile(1)).rearrange("p (g o) -> p g o", g=NNG).unsqueeze(2)
                        .broadcast_to([P, NNG, PH, CG]), ALU.add).then_inc(s_y32, 1)
                    wait(dve, s_yh, s.tile(2))
                    nc.vector.tensor_tensor(yl[:, :, :], act32[:, :, :], yh[:, :, :], ALU.subtract)\
                        .then_inc(s_yl, 1)
                if s.is_tile(-1):
                    for n in range(3, LAYER0 + 3):
                        split_low(n)
                        if n == 5:
                            split_x(s)
                if s.there(0):
                    wait(dve, s_acc[0], s.tile(1))
                    wait(dve, s_xb, s.tile(1))
                    wait(dve, s_o, s.tile(-1))
                    if s.is_tile(0):
                        dve.wait_ge(s_toep_l, 1)
                    nc.vector.scalar_tensor_tensor(out=x1[:, s.slot(), :], in0=acc[0][:, :], scalar=PSUM0,
                                                   in1=xb[:, s.slot(), :], op0=ALU.mult, op1=ALU.add)\
                        .then_inc(s_x1, 1)
                    wait(dve, s_aggh, s.tile(1))
                    for h in range(2):
                        a = nc.vector.scalar_tensor_tensor(
                            out=aggl[h * CH:(h + 1) * CH, h * CH:(h + 1) * CH], in0=agg_of(h, s.tile()),
                            scalar=S_AGG, in1=aggh[h * CH:(h + 1) * CH, h * CH:(h + 1) * CH],
                            op0=ALU.mult, op1=ALU.subtract)
                    a.then_inc(s_aggl, 1)
                    wait(dve, s_x1h, s.tile(1))
                    nc.vector.tensor_tensor(x1l[:, :], x1[:, s.slot(), :], x1h[:, :], ALU.subtract)\
                        .then_inc(s_x1l, 1)
                if s.is_tile(0):
                    for n in range(LAYER0 + 3, 2 * LAYER0):
                        split_low(n)
                if s.there(-1):
                    gate1(s)
                    wait(dve, s_hth[1], s.tile(0))
                    low(hwl[:, :], hwt[:, 0:D], hwh[:, :], S_HW, s_htl[1])

            nc.vector.memset(toep[:, :, :], 0.0).then_inc(s_zero, 1)
            for slot in range(2):
                nc.vector.memset(xs[:, slot, :, :, :], 0.0).then_inc(s_zero, 1)
            pipeline(dve, body, TILES // 2 - 1, (-1, 4))

        @block.tensor
        def _(pe):
            def gates(i, ah, al, width, k):
                for n, (a, w) in enumerate(((ah, 0), (ah, 1), (al, 0))):
                    m = nc.tensor.matmul(gat[:, 0:width], a[:, k, :], (w0, w1)[i][:, k, w, :][:, L:L + width],
                                         start=(k == 0 and n == 0), stop=(k == KT - 1 and n == 2))
                return m

            def base(i, ah, al, k):
                for n, (a, w) in enumerate(((ah, 0), (ah, 1), (al, 0))):
                    for h in range(2):
                        nc.tensor.matmul(acc[i][:, h * HALF:(h + 1) * HALF], a[:, k, :],
                                         (w0, w1)[i][:, k, w, :][:, h * HALF:(h + 1) * HALF],
                                         start=(k == 0 and n == 0), stop=False)

            def lora_b(i):
                for n, (a, w) in enumerate(((hwh, bh[i]), (hwh, bl[i]), (hwl, bh[i]))):
                    for h in range(2):
                        m = nc.tensor.matmul(acc[i][:, h * HALF:(h + 1) * HALF], a[:, :],
                                             w[:, h * HALF:(h + 1) * HALF], start=False, stop=(n == 2))
                m.then_inc(s_acc[i], 1)

            def turn_hw(i):
                nc.tensor.transpose(hwt[:, 0:D], hw[:, :], ident[:, :]).then_inc(s_ht[i], 1)

            def conv(s):
                for g in range(NNG):
                    c0 = (g % NGRP) * CG
                    for n, (part, band) in enumerate(((0, toep_h), (0, toep_l), (1, toep_h))):
                        for b in range(2):
                            m = nc.tensor.matmul(mix[:, g * P:(g + 1) * P],
                                                 xp[:, s.slot(1), g, part, b:b + P],
                                                 band[:, PH * b:PH * (b + 1), c0:c0 + CG],
                                                 start=(n == 0 and b == 0), stop=(n == 2 and b == 1))
                m.then_inc(s_conv, 1)

            def mixing():
                for j in range(KT):
                    for n, (a, w) in enumerate(((x1h, aggh), (x1h, aggl), (x1l, aggh))):
                        m = nc.tensor.matmul(mix[:, j * D:(j + 1) * D], a[:, j * P:(j + 1) * P], w[:, :],
                                             start=(n == 0), stop=(n == 2))
                m.then_inc(s_z, 1)

            def spread(n):
                if n >= 4:
                    pe.wait_ge(s_bcast_out, n)
                elif n >= 2:
                    pe.wait_ge(s_bcast_out, n - 1)
                for b in range(16):
                    k = 16 * (n % 4) + b
                    m = nc.tensor.matmul(bcast_acc(n)[:, b * CH:(b + 1) * CH],
                                         sel[:, k:k + 1].broadcast_to([P, P]), row16[:, n // 4, :],
                                         start=True, stop=True)
                m.then_inc(s_bcast, 1)

            def prelude():
                pe.wait_ge(s_cond, 16 * 3)
                nc.tensor.matmul(gat[0:NB, 128:128 + CH], embt[:, :], cwt[:, :], start=True, stop=True)\
                    .then_inc(s_row_mm, 1)
                pe.wait_ge(s_mlp, 16 * 6)
                nc.tensor.matmul(hwt[:, 0:NB], mw0[:, :], embt[:, :], start=True, stop=True).then_inc(s_mlp_mm, 1)
                pe.wait_ge(s_row, 3)
                pe.wait_ge(s_const, 5)
                pe.wait_ge(s_mlp_act, 1)
                nc.tensor.matmul(gat[:, 0:NB], mw1[:, :], h1[:, :], start=True, stop=True).then_inc(s_mlp_mm, 1)
                spread(0)
                spread(1)
                pe.wait_ge(s_mlp_act, 2)
                nc.tensor.matmul(hwt[0:NB, 256:256 + NK], h2[:, :], mw2[:, :], start=True, stop=True)\
                    .then_inc(s_mlp_mm, 1)

            def attention():
                pe.wait_ge(s_mlp_dve, 4)
                nc.tensor.transpose(gat[0:NK, 256:256 + NB], att[:, :], ident[0:NB, 0:NB]).then_inc(s_mlp_mm, 1)
                pe.wait_ge(s_mlp_dve, 5)
                pe.wait_ge(s_kern, 16 * 2)
                nc.tensor.matmul(gat[0:NB, 128:128 + CH], attt[:, :], kb[:, :], start=True, stop=True)\
                    .then_inc(s_row_mm, 1)
                pe.wait_ge(s_row, 6)

            def aggregate(r):
                if r == 0:
                    pe.wait_ge(s_bcast_out, 8)
                else:
                    pe.wait_ge(s_agg_out, r)
                for o in range(16):
                    c = 32 * r + 2 * o
                    m = nc.tensor.matmul(acc[1][:, o * NB:(o + 1) * NB],
                                         kw[:, c:c + 2, :].rearrange("k a i -> k (a i)"), attt[:, :],
                                         start=True, stop=True)
                m.then_inc(s_agg, 1)

            def body(s):
                if s.is_tile(-1):
                    prelude()
                if s.there(0):
                    wait(pe, s_yh, s.tile(1))
                    wait(pe, s_yl, s.tile(1))
                    if s.is_tile(0):
                        pe.wait_ge(s_bcast_out, 4)
                        for k in range(KT):
                            pe.wait_ge(s_split_h, k + 1)
                            pe.wait_ge(s_split_l, k + 1)
                            m = gates(0, yh, yl, G0W, k)
                            base(0, yh, yl, k)
                            if 2 <= k < 6:
                                spread(k + 2)
                            elif k >= 6:
                                aggregate(k - 6)
                        m.then_inc(s_g[0], 1)
                        pe.wait_ge(s_split_l, LAYER0)
                    else:
                        for k in range(KT):
                            m = gates(0, yh, yl, G0W, k)
                        m.then_inc(s_g[0], 1)
                        for k in range(KT):
                            base(0, yh, yl, k)
                    wait(pe, s_hw[0], s.tile(1))
                    turn_hw(0)
                if s.there(1):
                    if s.is_tile(0, 1):
                        pe.wait_ge(s_toep_l, 1)
                    wait(pe, s_xp[s.slot(1)], (s.pair(1) + 1) * 16 * NNG)
                    wait(pe, s_z32, s.tile(0))
                    conv(s)
                if s.is_tile(-1):
                    spread(2)
                    spread(3)
                    attention()
                if s.there(0):
                    wait(pe, s_hth[0], s.tile(1))
                    wait(pe, s_htl[0], s.tile(1))
                    lora_b(0)
                if s.there(-1):
                    wait(pe, s_zh, s.tile(0))
                    wait(pe, s_zl, s.tile(0))
                    if s.is_tile(0, -1):
                        pe.wait_ge(s_split_l, 2 * LAYER0)
                    wait(pe, s_o, s.tile(-1))
                    for k in range(KT):
                        m = gates(1, zh, zl, G1W, k)
                    m.then_inc(s_g[1], 1)
                    for k in range(KT):
                        base(1, zh, zl, k)
                    wait(pe, s_hw[1], s.tile(0))
                    turn_hw(1)
                if s.there(0):
                    wait(pe, s_x1h, s.tile(1))
                    wait(pe, s_x1l, s.tile(1))
                    wait(pe, s_aggl, s.tile(1))
                    if s.there(1):
                        wait(pe, s_y32, s.tile(2))
                    mixing()
                if s.there(-1):
                    wait(pe, s_hth[1], s.tile(0))
                    wait(pe, s_htl[1], s.tile(0))
                    lora_b(1)

            pipeline(pe, body, TILES // 2 - 1, (-1, 3))


def kernel(**inputs):
    import numpy as _np
    import concourse.bacc as _bacc
    from concourse import mybir as _mybir
    from concourse.bass_utils import run_bass_kernel_spmd as _run

    a = {k: _np.asarray(v) for k, v in inputs.items()}
    w0 = _np.concatenate([a["L0_ffn_W_base"], a["L0_ffn_lora_A"].reshape(ER, L), a["L0_ffn_W_router"]])
    w1 = _np.concatenate([a["L1_ffn_W_base"], a["L1_ffn_A_w"].reshape(ER, L), a["L1_ffn_W_gate"],
                          a["L1_ffn_W_thr"].reshape(1, L)])
    args = [
        ("x", a["x"].reshape(NB * CH, L)),
        ("emb_t", a["cond_128"].T),
        ("fside", a["fside_S_0"]),
        ("conv_w", a["L0_cond_weight"].transpose(1, 2, 0)),
        ("cw_t", a["L0_cond_c_weight"].T),
        ("w_l0", w0.reshape(L + G0W, P, PH)[:, :, ::-1].transpose(1, 2, 0)),
        ("lora_b0", a["L0_ffn_lora_B"].transpose(0, 2, 1).reshape(ER, L)),
        ("b_l0", a["L0_ffn_b_base"]),
        ("mlp_w0", a["L1_cond_W0"]),
        ("mlp_b0", a["L1_cond_b0"].reshape(HID, 1)),
        ("mlp_w1", a["L1_cond_W1"]),
        ("mlp_b1", a["L1_cond_b1"].reshape(HID, 1)),
        ("mlp_w2", a["L1_cond_W2"]),
        ("mlp_b2", a["L1_cond_b2"]),
        ("kern_w", a["L1_cond_weight"].reshape(NK, CH, CH)),
        ("kern_b", a["L1_cond_bias_k"]),
        ("w_l1", w1.reshape(L + G1W, KT, P).transpose(2, 1, 0)),
        ("lora_b1", a["L1_ffn_B_w"].transpose(0, 2, 1).reshape(ER, L)),
        ("b_l1", a["L1_ffn_b_base"]),
        ("b_thr", a["L1_ffn_b_thr"]),
    ]
    nc = _bacc.Bacc("TRN2", target_bir_lowering=False, num_devices=1)
    arrays, aps = {}, {}
    for name, v in args:
        v = _np.ascontiguousarray(v)
        arrays[f"{name}_dram"] = v
        aps[name] = nc.dram_tensor(f"{name}_dram", v.shape, _mybir.dt.from_np(v.dtype), kind="ExternalInput").ap()
    aps["out"] = nc.dram_tensor("out_dram", (NB * CH, L), _mybir.dt.float32, kind="ExternalOutput").ap()
    adaln_ffn(nc, **aps)
    r = _run(nc, [arrays], core_ids=[0])
    return r.results[0]["out_dram"].reshape(NB, CH, L)
```

```python
from contextlib import ExitStack

import concourse.bass as bass
from concourse import mybir

F32 = mybir.dt.float32
F16 = mybir.dt.float16
ALU = mybir.AluOpType
ACT = mybir.ActivationFunctionType
AX = mybir.AxisListType

P = 128
NB, CH, L = 64, 64, 1024
D = CH * 2
TILES = NB // 2
KT = L // P
PH = 8
NGRP, CG, TAPS = 4, 16, 9
NNG = 2 * NGRP
BLK = L // PH + 1
BLKP = BLK + 1
EXP, RANK = 8, 16
ER = EXP * RANK
CD, HID, NK = 128, 128, 8
KROW = CH * CH + CH
HALF = L // 2
G0W, G1W = ER + EXP, ER + EXP + 1
WROW = 1168
STAGES = 4

S_CONV = 4.0
S_W = 1024.0
S_AGG = 64.0
S_ATT = 1024.0
S_HW = 2.0 / S_W
PSUM0 = 1.0 / (S_CONV * S_W)
PSUM1 = 1.0 / S_W
PSUM_K = 1.0 / (S_ATT * S_W)
TINY = 1.1754944e-38
MAX_THR = 0.125


def wait(eng, sem, n):
    if isinstance(n, int) and n <= 0:
        return
    eng.wait_ge(sem, n)


class Step:

    def __init__(self, j, off, known=None):
        self.j, self.off, self.known = j, off, known

    def tile(self, d=0):
        return self.known[self.off + d] if self.known else self.j * 2 + self.off + d

    def pair(self, d=0):
        return self.j + (self.off + d) // 2

    def slot(self, d=0):
        return (self.off + d) % 2

    def there(self, d=0):
        return self.known is not None or 0 <= self.tile(d) < TILES

    def is_tile(self, n, d=0):
        return self.known is None and self.tile(d) == n


def pipeline(eng, body, loop_to, reach):
    for j in (-1, 0, 1):
        for off in (0, 1):
            body(Step(j, off))
    with eng.Fori(2, loop_to) as j:
        known = {n: j * 2 + n for n in range(reach[0], reach[1] + 1)}
        for count in known.values():
            eng.compute_val(count)
        for off in (0, 1):
            body(Step(j, off, known))
    for j in range(loop_to, TILES // 2 + 1):
        for off in (0, 1):
            body(Step(j, off))


def adaln_ffn(nc, x, cond_t, fside, conv_w, w_l0, lora_b0, b_l0, mlp_w, mlp_b2, kern,
              w_l1, lora_b1, b_l1, b_thr, out):
    with ExitStack() as ctx:
        def sb(name, shape, dt=F32, stack=ctx):
            return stack.enter_context(nc.sbuf_tensor(name, shape, dt))

        def sem(name):
            return ctx.enter_context(nc.semaphore(name))

        w0 = sb("w0", [P, KT, 2, WROW], F16)
        bh = [sb(f"b{i}h", [P, L], F16) for i in range(2)]
        bl = [sb(f"b{i}l", [P, L], F16) for i in range(2)]
        toep_h = sb("toep_h", [P, 2 * PH, CH], F16)
        toep_l = sb("toep_l", [P, 2 * PH, CH], F16)
        ctxb = sb("ctxb", [P, NB * CH])
        aggb = sb("aggb", [P, NB * CH])
        agg_t = sb("agg_t", [P, TILES, CH])
        row16 = sb("row16", [P, 2, CH], F16)
        brow = [sb(f"brow{i}", [P, L]) for i in range(2)]
        ident = sb("ident", [P, P])
        sel = sb("sel", [P, NB], F16)
        tie = sb("tie", [P, EXP, EXP])
        bthr = sb("bthr", [P, 1])
        nthr = sb("nthr", [P, 1])
        x_in = sb("x_in", [P, 2, L])
        xb_all = sb("xb_all", [P, 2 * L])
        xb = xb_all[:, :].rearrange("p (s l) -> p s l", s=2)
        xs = sb("xs", [P, 2, PH, 2, BLKP], F16)
        xp = sb("xp", [P, 2, NNG, 2, BLKP], F16)
        act32 = sb("act32", [P, KT, D])
        yh = sb("yh", [P, KT, D], F16)
        yl = sb("yl", [P, KT, D], F16)
        zh = sb("zh", [P, KT, D], F16)
        zl = sb("zl", [P, KT, D], F16)
        x1 = sb("x1", [P, 2, L])
        x1h = sb("x1h", [P, L], F16)
        x1l = sb("x1l", [P, L], F16)
        aggh = sb("aggh", [P, D], F16)
        aggl = sb("aggl", [P, D], F16)
        stage = sb("stage", [P, STAGES - 1, WROW])
        lg = sb("lg", [P, EXP + 1])
        nmax = sb("nmax", [P, 1])
        ex = sb("ex", [P, EXP])
        dif = sb("dif", [P, EXP, EXP])
        gtm = sb("gtm", [P, EXP, EXP])
        rank = sb("rank", [P, EXP])
        wsel = sb("wsel", [P, EXP])
        wsum = sb("wsum", [P, 2])
        wden = sb("wden", [P, 1])
        winv = sb("winv", [P, 2])
        thr = sb("thr", [P, 1])
        hw = sb("hw", [P, ER])
        hwh = sb("hwh", [P, D], F16)
        hwl = sb("hwl", [P, D], F16)

        with ExitStack() as pre:
            kern32 = sb("kern32", [P, KROW // 16], F32, pre)
            kern_h = sb("kern_h", [P, KROW // 16], F16, pre)
            kern_l = sb("kern_l", [P, KROW // 16], F16, pre)
            kern3 = sb("kern3", [3 * NK, KROW], F16, pre)
            cond = sb("cond", [CD, NB + CH], F32, pre)
            embt, cwt = cond[:, 0:NB], cond[:, NB:NB + CH]
            fsb = sb("fsb", [NB, CH], F32, pre)
            row32 = sb("row32", [NB, 2, CH], F32, pre)
            mlp = sb("mlp", [HID, 2 * HID + NK + 2], F32, pre)
            mw0, mw1, mw2 = mlp[:, 0:HID], mlp[:, HID:2 * HID], mlp[:, 2 * HID:2 * HID + NK]
            mb0, mb1 = (mlp[:, c:c + 1] for c in (2 * HID + NK, 2 * HID + NK + 1))
            mb2 = sb("mb2", [NB, NK], F32, pre)
            h1 = sb("h1", [HID, NB], F32, pre)
            h2 = sb("h2", [HID, NB], F32, pre)
            alg = sb("alg", [NB, NK], F32, pre)
            anm = sb("anm", [NB, 1], F32, pre)
            aex = sb("aex", [NB, NK], F32, pre)
            asum = sb("asum", [NB, 1], F32, pre)
            ainv = sb("ainv", [NB, 1], F32, pre)
            att = sb("att", [NB, 3, NK], F32, pre)
            atth = sb("atth", [NB, NK], F16, pre)
            attt = sb("attt", [3 * NK, NB], F16, pre)
        w1 = sb("w1", [P, KT, 2, WROW], F16)
        toep = x1[:, 0, :].rearrange("p (c o) -> p c o", o=CH)

        acc = [ctx.enter_context(nc.psum_tensor(f"acc{i}", [P, L], F32)) for i in range(2)]
        mix = ctx.enter_context(nc.psum_tensor("mix", [P, L], F32))
        gat = ctx.enter_context(nc.psum_tensor("gat", [P, HALF], F32))
        hwt = ctx.enter_context(nc.psum_tensor("hwt", [P, HALF], F32))

        s_zero = sem("s_zero")
        s_const = sem("s_const")
        s_toep = sem("s_toep")
        s_cond = sem("s_cond")
        s_mlp = sem("s_mlp")
        s_kern = sem("s_kern")
        s_kern_split = sem("s_kern_split")
        s_kern3 = sem("s_kern3")
        s_brow = [sem(f"s_brow{i}") for i in range(2)]
        s_bthr = sem("s_bthr")
        s_nthr = sem("s_nthr")
        s_toep_h = sem("s_toep_h")
        s_toep_l = sem("s_toep_l")
        s_row_mm = sem("s_row_mm")
        s_row = sem("s_row")
        s_bcast = sem("s_bcast")
        s_bcast_out = sem("s_bcast_out")
        s_mlp_mm = sem("s_mlp_mm")
        s_mlp_act = sem("s_mlp_act")
        s_mlp_dve = sem("s_mlp_dve")
        s_agg = sem("s_agg")
        s_agg_out = sem("s_agg_out")
        s_first = [sem(f"s_first{i}") for i in range(STAGES)]
        s_stage = [sem(f"s_stage{i}") for i in range(STAGES)]
        s_split_h = sem("s_split_h")
        s_split_l = sem("s_split_l")
        s_x = [sem(f"s_xin{i}") for i in range(2)]
        s_xh = sem("s_xh")
        s_xl = sem("s_xl")
        s_xp = [[sem(f"s_xp{i}{e}") for e in range(2)] for i in range(2)]
        s_xb = sem("s_xb")
        s_conv = sem("s_conv")
        s_y32 = sem("s_y32")
        s_yh = sem("s_yh")
        s_yl = sem("s_yl")
        s_g = [sem("s_g0"), sem("s_g1")]
        s_lg = [sem("s_lg0"), sem("s_lg1")]
        s_ex = [sem("s_ex0"), sem("s_ex1")]
        s_dve = sem("s_dve")
        s_hw = [sem("s_hw0"), sem("s_hw1")]
        s_ht = [sem("s_ht0"), sem("s_ht1")]
        s_hth = [sem("s_hth0"), sem("s_hth1")]
        s_htl = [sem("s_htl0"), sem("s_htl1")]
        s_acc = [sem("s_acc0"), sem("s_acc1")]
        s_x1 = sem("s_x1")
        s_x1h = sem("s_x1h")
        s_x1l = sem("s_x1l")
        s_x1b = sem("s_x1b")
        s_aggh = sem("s_aggh")
        s_aggl = sem("s_aggl")
        s_z = sem("s_z")
        s_z32 = sem("s_z32")
        s_zh = sem("s_zh")
        s_zl = sem("s_zl")
        s_o = sem("s_o")
        s_out = [sem(f"s_out{i}") for i in range(2)]

        def weights(src, dst, width):
            return [(src[:, k, :], dst[:, k, 0, 0:width], dst[:, k, 1, 0:width], width) for k in range(KT)]

        lora = [(b, bh[i][:, :], bl[i][:, :], L) for i, b in enumerate((lora_b0, lora_b1))]
        first, second = weights(w_l0, w0, L + G0W), weights(w_l1, w1, L + G1W)
        pieces = first + lora[:1] + second[5:] + lora[1:] + second[:5]
        LAYER0 = KT + 1
        CLEAR = LAYER0 + 4
        slots = [n % STAGES if n < LAYER0 else (n + 1) % (STAGES - 1) for n in range(len(pieces))]
        LAST_IN_XB = max(n for n in range(len(pieces)) if slots[n] == STAGES - 1)

        def staged(n):
            width = pieces[n][3]
            return stage[:, slots[n], 0:width] if slots[n] < STAGES - 1 else xb_all[:, 0:width]

        def landed(eng, n):
            if n < STAGES:
                eng.wait_ge(s_first[n], 16)
            else:
                eng.wait_ge(s_stage[slots[n]], 16 * slots[STAGES:n + 1].count(slots[n]))

        def put_stage(eng, n):
            before = [m for m in range(n) if slots[m] == slots[n]]
            if before:
                eng.wait_ge(s_split_h, before[-1] + 1)
                eng.wait_ge(s_split_l, before[-1] + 1)
            eng.dma_start(staged(n), pieces[n][0]).then_inc((s_stage if before else s_first)[slots[n]], 16)

        def spreads(s):
            return s.is_tile(1) or s.is_tile(2) or s.is_tile(3)

        def out_parts(s):
            return ((0, HALF), (HALF, L)) if s.is_tile(TILES - 1, -2) else ((0, L),)

        def early(s):
            return any(s.is_tile(n) for n in (-2, -1, 0, 1))

        def by_phase(slot):
            v = x_in[:, slot, :].rearrange("p (b f) -> p f b", f=PH)
            return ((v[:, PH // 2:PH, :], 0, PH // 2, 1), (v[:, 0:PH // 2, :], PH // 2, PH, 0))

        conv_out = mix[:, :].rearrange("p (g c o) -> p g c o", g=NNG, c=PH)
        y_out = act32[:, :, :].rearrange("p c (g o) -> p g c o", g=NNG)

        def row_of(tab, n):
            return tab[:, bass.ds(n * D, D)] if not isinstance(n, int) else tab[:, n * D:(n + 1) * D]

        def agg_of(h, n):
            part = agg_t[h * CH:(h + 1) * CH, bass.ds(n, 1), :] if not isinstance(n, int) else \
                agg_t[h * CH:(h + 1) * CH, n:n + 1, :]
            return part.rearrange("p a o -> p (a o)")

        def rows(ap, n):
            return ap[bass.ds(n * D, D), :] if not isinstance(n, int) else ap[n * D:(n + 1) * D, :]

        block = ctx.enter_context(nc.Block())

        @block.sync
        def _(sp):
            def load_x(slot, n):
                sp.dma_start(x_in[:, slot, :], rows(x, n)).then_inc(s_x[slot], 16)

            load_x(0, 0)
            sp.dma_start(cond[:, :], cond_t).then_inc(s_cond, 16)
            sp.dma_start(x1[:, 0, :], bass.AP(conv_w.tensor, conv_w.offset, [
                [conv_w.shape[1] * CH, CG], [CH, PH], [1, 2 * PH * CH]])).then_inc(s_toep, 16)
            sp.dma_start(fsb[:, :], fside.partition_broadcast(NB)).then_inc(s_cond, 16)

            def body(s):
                if s.there(-2):
                    wait(sp, s_o, s.tile(-1))
                if s.is_tile(0):
                    for n in range(LAYER0 + 3, LAYER0 + 7):
                        put_stage(sp, n)
                if s.known:
                    wait(sp, s_xb, s.tile(2))
                if s.there(2):
                    wait(sp, s_xh, s.tile(3))
                    wait(sp, s_xl, s.tile(3))
                    wait(sp, s_conv, s.tile(1))
                    for g in range(NNG):
                        sp.dma_start(xp[:, s.slot(), g, :, :].rearrange("p h b -> p (h b)"),
                                     xs[g * CG:(g + 1) * CG, s.slot(), :, :, :]
                                     .rearrange("i f h b -> i f (h b)")).then_inc(s_xp[s.slot()][g // NGRP], 16)
                if s.is_tile(0):
                    for n in range(LAYER0 + 7, 2 * LAYER0):
                        put_stage(sp, n)
                if s.is_tile(-2):
                    for n in range(2, LAYER0):
                        put_stage(sp, n)
                        if n == STAGES:
                            load_x(1, 1)
                if s.is_tile(-1):
                    for n in range(LAYER0, LAYER0 + 3):
                        put_stage(sp, n)
                if s.there(-2):
                    for n, (c0, c1) in enumerate(out_parts(s)):
                        if n:
                            wait(sp, s_o, s.tile(-1) + n)
                        sp.dma_start(rows(out, s.tile(-2))[:, c0:c1], stage[:, s.slot(), c0:c1])\
                            .then_inc(s_out[s.slot()], 16)
                if s.there(3) and not s.is_tile(1, 3):
                    if not s.known:
                        wait(sp, s_xb, s.tile(2))
                    load_x(s.slot(3), s.tile(3))

            pipeline(sp, body, TILES // 2 - 2, (-2, 4))
            sp.wait_ge(s_out[0], 16 * (TILES // 2))
            sp.wait_ge(s_out[1], 16 * (TILES // 2 + 1))

        @block.gpsimd
        def _(pool):
            for dst, src in ((mlp, mlp_w), (mb2, mlp_b2.partition_broadcast(NB))):
                pool.dma_start(dst[:, :], src).then_inc(s_mlp, 16)
            put_stage(pool, 0)
            nc.gpsimd.memset(sel[:, :], 0.0).then_inc(s_const, 1)
            nc.gpsimd.memset(ident[:, :], 0.0).then_inc(s_const, 1)
            pool.wait_ge(s_const, 2)
            for h in range(2):
                nc.gpsimd.affine_select(out=sel[:, :], in_=sel[:, :], compare_op=ALU.not_equal, fill=1.0,
                                        base=-h * NB, pattern=[[-1, NB]], channel_multiplier=1)\
                    .then_inc(s_const, 1)
                pool.wait_ge(s_const, 3 + h)
            nc.gpsimd.affine_select(out=ident[:, :], in_=ident[:, :], compare_op=ALU.not_equal, fill=1.0,
                                    base=0, pattern=[[-1, P]], channel_multiplier=1).then_inc(s_const, 1)
            pool.dma_start(kern32[:, :], kern).then_inc(s_kern, 16)
            put_stage(pool, 1)
            pool.wait_ge(s_kern_split, 2)
            for part, src in enumerate((kern_h, kern_l, kern_h)):
                pool.dma_start(kern3[part * NK:(part + 1) * NK, :].rearrange("k (a b) -> k a b", a=16),
                               src[:, :]).then_inc(s_kern3, 16)
            nc.gpsimd.memset(tie[:, :, :], 0.0).then_inc(s_const, 1)
            nc.gpsimd.memset(aggh[:, :], 0.0).then_inc(s_const, 1)
            nc.gpsimd.memset(aggl[:, :], 0.0).then_inc(s_const, 1)
            pool.wait_ge(s_const, 6)
            nc.gpsimd.affine_select(out=tie[:, :, :], in_=tie[:, :, :], compare_op=ALU.is_ge, fill=-TINY,
                                    base=0, pattern=[[-1, EXP], [1, EXP]], channel_multiplier=0)\
                .then_inc(s_const, 1)
            pool.dma_start(bthr[:, :], b_thr.partition_broadcast(P)).then_inc(s_bthr, 16)
            pool.wait_ge(s_split_h, 6)
            pool.dma_start(brow[0][:, :], b_l0.partition_broadcast(P)).then_inc(s_brow[0], 16)
            pool.wait_ge(s_xp[1][1], 16 * NGRP)
            pool.dma_start(brow[1][:, :], b_l1.partition_broadcast(P)).then_inc(s_brow[1], 16)

            def body(s):
                if s.there(0):
                    wait(pool, s_x1, s.tile(1))
                    wait(pool, s_x1h, s.tile(1))
                    wait(pool, s_x1l, s.tile(1))
                    if s.is_tile(0):
                        pool.wait_ge(s_brow[1], 16)
                    nc.gpsimd.tensor_tensor(x1[:, s.slot(), :], x1[:, s.slot(), :], brow[1][:, :], ALU.add)\
                        .then_inc(s_x1b, 1)
                if s.there(2):
                    wait(pool, s_x[s.slot()], (s.pair(2) + 1) * 16)
                    wait(pool, s_x1, s.tile(1))
                    if s.is_tile(0, 2):
                        pool.wait_ge(s_brow[0], 16)
                        pool.wait_ge(s_split_h, LAST_IN_XB + 1)
                        pool.wait_ge(s_split_l, LAST_IN_XB + 1)
                    nc.gpsimd.tensor_tensor(xb[:, s.slot(), :], x_in[:, s.slot(), :], brow[0][:, :], ALU.add)\
                        .then_inc(s_xb, 1)

            pipeline(pool, body, TILES // 2 - 1, (1, 4))

        @block.scalar
        def _(act):
            def split_high(n):
                if n == CLEAR:
                    act.wait_ge(s_agg, 2)
                landed(act, n)
                nc.scalar.activation(pieces[n][1], staged(n), ACT.Copy, scale=S_W).then_inc(s_split_h, 1)

            def rows_out(n):
                act.wait_ge(s_bcast, n + 1)
                k = n // 2
                nc.scalar.activation((ctxb, aggb)[n % 2][:, k * L:(k + 1) * L], acc[1][:, :], ACT.Copy)\
                    .then_inc(s_bcast_out, 1)

            def agg_out(r):
                act.wait_ge(s_agg, r + 1)
                for q in range(2):
                    for e in range(2):
                        src = acc[1][q * CH:(q + 1) * CH, :].rearrange("p (o b) -> p b o", b=NB)
                        a = nc.scalar.activation(agg_t[e * CH:(e + 1) * CH, :, 32 * r + q:32 * r + 32:2],
                                                 src[:, e:NB:2, :], ACT.Copy, scale=PSUM_K)
                a.then_inc(s_agg_out, 1)

            def split_x(s):
                wait(act, s_x[s.slot()], (s.pair(2) + 1) * 16)
                if s.there(0):
                    for e in range(2):
                        wait(act, s_xp[s.slot()][e], (s.pair() + 1) * 16 * NGRP)
                for src, f0, f1, b0 in by_phase(s.slot()):
                    a = nc.scalar.activation(xs[:, s.slot(), f0:f1, 0, b0:b0 + BLK - 1], src, ACT.Copy)
                a.then_inc(s_xh, 1)

            def prelude():
                act.wait_ge(s_mlp, 16 * 2)
                act.wait_ge(s_mlp_mm, 1)
                nc.scalar.activation(h1[:, :], hwt[:, 0:NB], ACT.Gelu, bias=mb0[:, 0:1]).then_inc(s_mlp_act, 1)
                act.wait_ge(s_toep, 16)
                nc.scalar.activation(toep_h[:, :, :], toep[:, :, :], ACT.Copy, scale=S_CONV).then_inc(s_toep_h, 1)
                act.wait_ge(s_mlp_mm, 2)
                nc.scalar.activation(h2[:, :], gat[:, 0:NB], ACT.Gelu, bias=mb1[:, 0:1]).then_inc(s_mlp_act, 1)
                rows_out(0)
                split_high(0)
                split_high(1)
                act.wait_ge(s_mlp_dve, 2)
                nc.scalar.activation(aex[:, :], alg[:, :], ACT.Exp, bias=anm[:, 0:1], accum_out=asum[:, 0:1])\
                    .then_inc(s_mlp_act, 1)
                split_high(2)

            def body(s):
                def z_high():
                    wait(act, s_z32, s.tile(0))
                    nc.scalar.activation(zh[:, :, :], act32[:, :, :], ACT.Copy).then_inc(s_zh, 1)

                if s.there(-1) and not s.is_tile(1):
                    z_high()
                if s.there(0):
                    wait(act, s_lg[0], s.tile(1))
                    nc.scalar.activation(ex[:, :], lg[:, 0:EXP], ACT.Exp, bias=nmax[:, 0:1])\
                        .then_inc(s_ex[0], 1)
                if spreads(s):
                    rows_out(2 * s.tile())
                if s.is_tile(1):
                    z_high()
                    split_high(LAYER0 + 5)
                if s.there(2) and not early(s):
                    split_x(s)
                if s.is_tile(-2):
                    prelude()
                if s.there(0):
                    wait(act, s_ht[0], s.tile(1))
                    nc.scalar.activation(hwh[:, :], hwt[:, 0:D], ACT.Copy, scale=S_HW).then_inc(s_hth[0], 1)
                if spreads(s):
                    rows_out(2 * s.tile() + 1)
                if s.is_tile(0):
                    split_high(LAYER0)
                if s.is_tile(1):
                    for n in range(LAYER0 + 6, LAYER0 + 8):
                        split_high(n)
                if s.there(1):
                    wait(act, s_y32, s.tile(2))
                    nc.scalar.activation(yh[:, :, :], act32[:, :, :], ACT.Copy).then_inc(s_yh, 1)
                if s.is_tile(0):
                    split_high(LAYER0 + 1)
                    agg_out(1)
                if s.is_tile(-1):
                    for n in range(3, 6):
                        split_high(n)
                    rows_out(1)
                    split_x(s)
                    split_high(6)
                    split_high(7)
                    agg_out(0)
                    split_high(8)
                if s.there(0):
                    if s.is_tile(0):
                        act.wait_ge(s_agg_out, 2)
                        act.wait_ge(s_const, 8)
                    else:
                        wait(act, s_z, s.tile(0))
                    for h in range(2):
                        a = nc.scalar.activation(aggh[h * CH:(h + 1) * CH, h * CH:(h + 1) * CH],
                                                 agg_of(h, s.tile()), ACT.Copy, scale=S_AGG)
                    a.then_inc(s_aggh, 1)
                    if s.is_tile(1):
                        split_high(2 * LAYER0 - 1)
                    wait(act, s_x1, s.tile(1))
                    nc.scalar.activation(x1h[:, :], x1[:, s.slot(), :], ACT.Copy).then_inc(s_x1h, 1)
                if s.is_tile(0):
                    for n in range(LAYER0 + 2, LAYER0 + 4):
                        split_high(n)
                    split_x(s)
                    split_high(LAYER0 + 4)
                if s.there(-1):
                    wait(act, s_lg[1], s.tile(0))
                    nc.scalar.activation(ex[:, :], lg[:, 0:EXP], ACT.Exp, bias=nmax[:, 0:1],
                                         accum_out=wsum[:, 0:1]).then_inc(s_ex[1], 1)
                    if s.is_tile(1):
                        act.wait_ge(s_nthr, 1)
                    nc.scalar.activation(wsum[:, 1:2], lg[:, EXP:EXP + 1], ACT.Exp, scale=-1.0,
                                         bias=nthr[:, 0:1]).then_inc(s_ex[1], 1)
                    if s.is_tile(1):
                        split_x(s)
                    wait(act, s_ht[1], s.tile(0))
                    nc.scalar.activation(hwh[:, :], hwt[:, 0:D], ACT.Copy, scale=S_HW).then_inc(s_hth[1], 1)

            pipeline(act, body, TILES // 2 - 1, (-1, 4))

        @block.vector
        def _(dve):
            def low(dst, full, high, scale, done):
                return nc.vector.scalar_tensor_tensor(out=dst, in0=full, scalar=scale, in1=high,
                                                      op0=ALU.mult, op1=ALU.subtract).then_inc(done, 1)

            def split_low(n):
                dve.wait_ge(s_split_h, n + 1)
                low(pieces[n][2], staged(n), pieces[n][1], S_W, s_split_l)

            def split_rows(n):
                dve.wait_ge(s_row_mm, n + 1)
                src = (gat[0:NB, 128:128 + CH], hwt[0:NB, 128:128 + CH])[n]
                scale = (S_CONV, 1.0)[n]
                if n == 0:
                    dve.wait_ge(s_cond, 16 * 2)
                    nc.vector.tensor_tensor(row32[:, n, :], src, fsb[:, :], ALU.add)\
                        .then_inc(s_row, 1)
                else:
                    nc.vector.tensor_scalar(row32[:, n, :], src, PSUM_K, None, ALU.mult).then_inc(s_row, 1)
                dve.wait_ge(s_row, 3 * n + 1)
                nc.vector.tensor_scalar(row16[0:NB, n, :], row32[:, n, :], scale, None, ALU.mult)\
                    .then_inc(s_row, 1)
                dve.wait_ge(s_row, 3 * n + 2)
                low(row16[NB:P, n, :], row32[:, n, :], row16[0:NB, n, :], scale, s_row)

            def prelude():
                dve.wait_ge(s_kern, 16)
                nc.vector.tensor_scalar(kern_h[:, :], kern32[:, :], S_W, None, ALU.mult).then_inc(s_kern_split, 1)
                dve.wait_ge(s_kern_split, 1)
                low(kern_l[:, :], kern32[:, :], kern_h[:, :], S_W, s_kern_split)
                dve.wait_ge(s_toep_h, 1)
                low(toep_l[:, :, :], toep[:, :, :], toep_h[:, :, :], S_CONV, s_toep_l)
                dve.wait_ge(s_mlp_mm, 3)
                nc.vector.tensor_tensor(alg[:, :], hwt[0:NB, 256:256 + NK], mb2[:, :], ALU.add)\
                    .then_inc(s_mlp_dve, 1)
                dve.wait_ge(s_mlp_dve, 1)
                nc.vector.tensor_reduce(anm[:, :], alg[:, :], AX.X, ALU.max, negate=True).then_inc(s_mlp_dve, 1)
                split_low(0)
                split_low(1)

            def attention():
                dve.wait_ge(s_mlp_act, 3)
                nc.vector.reciprocal(ainv[:, :], asum[:, :]).then_inc(s_mlp_dve, 1)
                dve.wait_ge(s_mlp_dve, 3)
                nc.vector.tensor_scalar(att[:, 0:2, :], aex[:, :].unsqueeze(1).broadcast_to([NB, 2, NK]),
                                        ainv[:, 0:1], S_ATT, ALU.mult, ALU.mult).then_inc(s_mlp_dve, 1)
                dve.wait_ge(s_mlp_dve, 4)
                nc.vector.tensor_copy(atth[:, :], att[:, 0, :]).then_inc(s_mlp_dve, 1)
                dve.wait_ge(s_mlp_dve, 5)
                nc.vector.tensor_tensor(att[:, 2, :], att[:, 0, :], atth[:, :], ALU.subtract)\
                    .then_inc(s_mlp_dve, 1)

            def split_x(s):
                wait(dve, s_xh, s.tile(3))
                for src, f0, f1, b0 in by_phase(s.slot()):
                    a = nc.vector.tensor_tensor(xs[:, s.slot(), f0:f1, 1, b0:b0 + BLK - 1], src,
                                                xs[:, s.slot(), f0:f1, 0, b0:b0 + BLK - 1], ALU.subtract)
                a.then_inc(s_xl, 1)

            def y_add(s):
                wait(dve, s_conv, s.tile(2))
                nc.vector.tensor_tensor(
                    y_out, conv_out,
                    row_of(ctxb, s.tile(1)).rearrange("p (g o) -> p g o", g=NNG).unsqueeze(2)
                    .broadcast_to([P, NNG, PH, CG]), ALU.add).then_inc(s_y32, 1)

            DEPTH0, DEPTH1 = 6, 9

            def gate0(s):
                t0 = s.tile() * (DEPTH0 + DEPTH1) - DEPTH1
                if s.is_tile(0):
                    t0 = 0
                wait(dve, s_g[0], s.tile(1))
                nc.vector.tensor_scalar(lg[:, 0:EXP], gat[:, ER:ER + EXP], PSUM0, None, ALU.mult)\
                    .then_inc(s_dve, 1)
                dve.wait_ge(s_dve, t0 + 1)
                nc.vector.tensor_reduce(nmax[:, :], lg[:, 0:EXP], AX.X, ALU.max, negate=True)\
                    .then_inc(s_lg[0], 1)
                wait(dve, s_ex[0], s.tile(1))
                nc.vector.tensor_tensor(dif[:, :, :], ex[:, :].unsqueeze(1).broadcast_to([P, EXP, EXP]),
                                        ex[:, :].unsqueeze(2).broadcast_to([P, EXP, EXP]), ALU.subtract)\
                    .then_inc(s_dve, 1)
                if s.is_tile(0):
                    dve.wait_ge(s_const, 9)
                dve.wait_ge(s_dve, t0 + 2)
                nc.vector.tensor_tensor(gtm[:, :, :], dif[:, :, :], tie[:, :, :], ALU.is_gt).then_inc(s_dve, 1)
                dve.wait_ge(s_dve, t0 + 3)
                nc.vector.tensor_reduce(rank[:, :], gtm[:, :, :], AX.X, ALU.add).then_inc(s_dve, 1)
                dve.wait_ge(s_dve, t0 + 4)
                nc.vector.scalar_tensor_tensor(out=wsel[:, :], in0=rank[:, :], scalar=1.5, in1=ex[:, :],
                                               op0=ALU.is_lt, op1=ALU.mult, accum_out=wden[:, :])\
                    .then_inc(s_dve, 1)
                dve.wait_ge(s_dve, t0 + 5)
                nc.vector.reciprocal(winv[:, 0:1], wden[:, :]).then_inc(s_dve, 1)
                dve.wait_ge(s_dve, t0 + 6)
                weigh(0)

            def weigh(i):
                nc.vector.scalar_tensor_tensor(
                    out=hw[:, :].rearrange("p (e r) -> p e r", e=EXP),
                    in0=gat[:, 0:ER].rearrange("p (e r) -> p e r", e=EXP), scalar=winv[:, 0:1],
                    in1=wsel[:, :].unsqueeze(2).broadcast_to([P, EXP, RANK]),
                    op0=ALU.mult, op1=ALU.mult).then_inc(s_hw[i], 1)

            def gate1(s):
                t0 = s.tile() * (DEPTH0 + DEPTH1) + DEPTH0 - DEPTH1
                if not s.there(0):
                    t0 = TILES * DEPTH0 + s.tile(-1) * DEPTH1
                wait(dve, s_g[1], s.tile(0))
                nc.vector.tensor_scalar(lg[:, :], gat[:, ER:ER + EXP + 1], PSUM1, None, ALU.mult)\
                    .then_inc(s_dve, 1)
                dve.wait_ge(s_dve, t0 + 1)
                nc.vector.tensor_reduce(nmax[:, :], lg[:, 0:EXP], AX.X, ALU.max, negate=True)\
                    .then_inc(s_lg[1], 1)
                wait(dve, s_ex[1], s.tile(0) * 2)
                nc.vector.tensor_scalar(wsum[:, 1:2], wsum[:, 1:2], 1.0, None, ALU.add).then_inc(s_dve, 1)
                dve.wait_ge(s_dve, t0 + 2)
                nc.vector.reciprocal(winv[:, :], wsum[:, :]).then_inc(s_dve, 1)
                dve.wait_ge(s_dve, t0 + 3)
                nc.vector.tensor_scalar(thr[:, :], winv[:, 1:2], MAX_THR, None, ALU.mult).then_inc(s_dve, 1)
                dve.wait_ge(s_dve, t0 + 4)
                nc.vector.tensor_scalar(rank[:, :], ex[:, :], winv[:, 0:1], thr[:, 0:1], ALU.mult,
                                        ALU.subtract).then_inc(s_dve, 1)
                dve.wait_ge(s_dve, t0 + 5)
                nc.vector.tensor_scalar(wsel[:, :], rank[:, :], 0.0, None, ALU.max).then_inc(s_dve, 1)
                dve.wait_ge(s_dve, t0 + 6)
                nc.vector.tensor_reduce(wden[:, :], wsel[:, :], AX.X, ALU.add).then_inc(s_dve, 1)
                dve.wait_ge(s_dve, t0 + 7)
                nc.vector.scalar_tensor_tensor(out=thr[:, :], in0=wden[:, :], scalar=0.0, in1=wden[:, :],
                                               op0=ALU.is_equal, op1=ALU.add).then_inc(s_dve, 1)
                dve.wait_ge(s_dve, t0 + 8)
                nc.vector.reciprocal(winv[:, 0:1], thr[:, :]).then_inc(s_dve, 1)
                dve.wait_ge(s_dve, t0 + 9)
                weigh(1)

            def body(s):
                def z_add(d=0):
                    wait(dve, s_z, s.tile(d))
                    if s.there(0) and not d:
                        wait(dve, s_yl, s.tile(1))
                    nc.vector.scalar_tensor_tensor(
                        out=act32[:, :, :], in0=mix[:, :].rearrange("p (j n) -> p j n", n=D),
                        scalar=1.0 / S_AGG,
                        in1=row_of(aggb, s.tile(d - 1)).unsqueeze(1).broadcast_to([P, KT, D]),
                        op0=ALU.mult, op1=ALU.add).then_inc(s_z32, 1)

                def z_low():
                    wait(dve, s_zh, s.tile(0))
                    nc.vector.tensor_tensor(zl[:, :, :], act32[:, :, :], zh[:, :, :], ALU.subtract)\
                        .then_inc(s_zl, 1)

                if s.there(-1) and not s.is_tile(1) and not s.is_tile(TILES):
                    z_add()
                if s.is_tile(TILES):
                    z_low()
                if s.there(-2):
                    wait(dve, s_acc[1], s.tile(-1))
                    wait(dve, s_x1b, s.tile(-1))
                    if s.is_tile(2) or s.is_tile(3):
                        dve.wait_ge(s_split_l, 2 * LAYER0)
                    if s.there(-4):
                        wait(dve, s_out[s.slot()], s.pair(-2) * 16)
                    for c0, c1 in out_parts(s):
                        nc.vector.scalar_tensor_tensor(
                            out=stage[:, s.slot(), c0:c1], in0=acc[1][:, c0:c1], scalar=PSUM1,
                            in1=x1[:, s.slot(), c0:c1], op0=ALU.mult, op1=ALU.add).then_inc(s_o, 1)
                if s.there(0):
                    gate0(s)
                if s.is_tile(1):
                    z_add()
                if s.there(-1) and not s.is_tile(TILES):
                    z_low()
                if s.is_tile(1):
                    split_low(LAYER0 + 5)
                if s.there(2) and (not early(s) or s.is_tile(0, 2)):
                    split_x(s)
                if s.is_tile(-2):
                    split_rows(0)
                    prelude()
                if s.is_tile(0):
                    dve.wait_ge(s_yl, 1)
                    y_add(s)
                if s.there(0):
                    wait(dve, s_hth[0], s.tile(1))
                    low(hwl[:, :], hwt[:, 0:D], hwh[:, :], S_HW, s_htl[0])
                if s.is_tile(0):
                    split_low(LAYER0)
                if s.is_tile(1):
                    for n in range(LAYER0 + 6, LAYER0 + 8):
                        split_low(n)
                if s.there(1):
                    if s.is_tile(-1):
                        dve.wait_ge(s_bcast_out, 1)
                    if not s.is_tile(0):
                        wait(dve, s_zl, s.tile(0))
                        y_add(s)
                    if s.is_tile(-1):
                        attention()
                    wait(dve, s_yh, s.tile(2))
                    nc.vector.tensor_tensor(yl[:, :, :], act32[:, :, :], yh[:, :, :], ALU.subtract)\
                        .then_inc(s_yl, 1)
                if s.is_tile(-1):
                    dve.wait_ge(s_mlp_mm, 4)
                    nc.vector.tensor_copy(attt[:, :], hwt[0:3 * NK, 256:256 + NB]).then_inc(s_mlp_dve, 1)
                    split_low(2)
                    split_low(3)
                    split_rows(1)
                    split_low(4)
                    split_low(5)
                    split_x(s)
                    for n in range(6, LAYER0):
                        split_low(n)
                if s.there(0):
                    wait(dve, s_acc[0], s.tile(1))
                    wait(dve, s_xb, s.tile(1))
                    wait(dve, s_o, s.tile(-1))
                    if s.is_tile(0):
                        dve.wait_ge(s_toep_l, 1)
                    nc.vector.scalar_tensor_tensor(out=x1[:, s.slot(), :], in0=acc[0][:, :], scalar=PSUM0,
                                                   in1=xb[:, s.slot(), :], op0=ALU.mult, op1=ALU.add)\
                        .then_inc(s_x1, 1)
                    wait(dve, s_aggh, s.tile(1))
                    for h in range(2):
                        a = nc.vector.scalar_tensor_tensor(
                            out=aggl[h * CH:(h + 1) * CH, h * CH:(h + 1) * CH], in0=agg_of(h, s.tile()),
                            scalar=S_AGG, in1=aggh[h * CH:(h + 1) * CH, h * CH:(h + 1) * CH],
                            op0=ALU.mult, op1=ALU.subtract)
                    a.then_inc(s_aggl, 1)
                    if s.is_tile(0):
                        split_low(LAYER0 + 1)
                    if s.is_tile(1):
                        split_low(2 * LAYER0 - 1)
                    wait(dve, s_x1h, s.tile(1))
                    nc.vector.tensor_tensor(x1l[:, :], x1[:, s.slot(), :], x1h[:, :], ALU.subtract)\
                        .then_inc(s_x1l, 1)
                if s.is_tile(0):
                    for n in range(LAYER0 + 2, LAYER0 + 4):
                        split_low(n)
                    split_x(s)
                    split_low(LAYER0 + 4)
                    dve.wait_ge(s_bthr, 16)
                    nc.vector.tensor_scalar(nthr[:, :], bthr[:, :], -1.0, None, ALU.mult).then_inc(s_nthr, 1)
                if s.there(-1):
                    gate1(s)
                    if s.is_tile(1):
                        split_x(s)
                    if s.is_tile(TILES - 1):
                        wait(dve, s_zl, s.tile(0))
                        z_add(1)
                    wait(dve, s_hth[1], s.tile(0))
                    low(hwl[:, :], hwt[:, 0:D], hwh[:, :], S_HW, s_htl[1])

            for b0, b1 in ((0, 1), (BLK - 1, BLKP)):
                nc.vector.memset(xs[:, :, :, :, b0:b1], 0.0).then_inc(s_zero, 1)
            dve.wait_ge(s_zero, 2)
            dve.wait_ge(s_x[0], 16)
            for src, f0, f1, b0 in by_phase(0):
                a = nc.vector.tensor_copy(xs[:, 0, f0:f1, 0, b0:b0 + BLK - 1], src)
            a.then_inc(s_xh, 1)
            pipeline(dve, body, TILES // 2 - 1, (-1, 4))

        @block.tensor
        def _(pe):
            def gates(i, ah, al, width, k, first=0, last=KT - 1):
                for n, (a, w) in enumerate(((ah, 0), (ah, 1), (al, 0))):
                    m = nc.tensor.matmul(gat[:, 0:width], a[:, k, :], (w0, w1)[i][:, k, w, :][:, L:L + width],
                                         start=(k == first and n == 0), stop=(k == last and n == 2))
                return m

            def base(i, ah, al, k, first=0):
                for n, (a, w) in enumerate(((ah, 0), (ah, 1), (al, 0))):
                    for h in range(2):
                        nc.tensor.matmul(acc[i][:, h * HALF:(h + 1) * HALF], a[:, k, :],
                                         (w0, w1)[i][:, k, w, :][:, h * HALF:(h + 1) * HALF],
                                         start=(k == first and n == 0), stop=False)

            def lora_b(i):
                for n, (a, w) in enumerate(((hwh, bh[i]), (hwh, bl[i]), (hwl, bh[i]))):
                    for h in range(2):
                        m = nc.tensor.matmul(acc[i][:, h * HALF:(h + 1) * HALF], a[:, :],
                                             w[:, h * HALF:(h + 1) * HALF], start=False, stop=(n == 2))
                m.then_inc(s_acc[i], 1)

            def turn_hw(s, i):
                wait(pe, s_hw[i], s.tile(1 - i))
                nc.tensor.transpose(hwt[:, 0:D], hw[:, :], ident[:, :]).then_inc(s_ht[i], 1)

            def conv(s):
                for g in range(NNG):
                    if g % NGRP == 0:
                        wait(pe, s_xp[s.slot(1)][g // NGRP], (s.pair(1) + 1) * 16 * NGRP)
                    c0 = (g % NGRP) * CG
                    for n, (part, band) in enumerate(((0, toep_h), (0, toep_l), (1, toep_h))):
                        for b in range(2):
                            m = nc.tensor.matmul(mix[:, g * P:(g + 1) * P],
                                                 xp[:, s.slot(1), g, part, b:b + P],
                                                 band[:, PH * b:PH * (b + 1), c0:c0 + CG],
                                                 start=(n == 0 and b == 0), stop=(n == 2 and b == 1))
                m.then_inc(s_conv, 1)

            def mixing():
                for j in range(KT):
                    for n, (a, w) in enumerate(((x1h, aggh), (x1h, aggl), (x1l, aggh))):
                        m = nc.tensor.matmul(mix[:, j * D:(j + 1) * D], a[:, j * P:(j + 1) * P], w[:, :],
                                             start=(n == 0), stop=(n == 2))
                m.then_inc(s_z, 1)

            def spread(n):
                if n >= 1:
                    pe.wait_ge(s_bcast_out, n)
                if n == 1:
                    pe.wait_ge(s_row, 6)
                if n == 2:
                    pe.wait_ge(s_agg_out, 2)
                if n in (4, 6):
                    pe.wait_ge(s_o, n // 2 - 1)
                for b in range(16):
                    k = 16 * (n // 2) + b
                    m = nc.tensor.matmul(acc[1][:, b * CH:(b + 1) * CH],
                                         sel[:, k:k + 1].broadcast_to([P, P]), row16[:, n % 2, :],
                                         start=True, stop=True)
                m.then_inc(s_bcast, 1)

            def next_conv(s):
                wait(pe, s_z32, s.tile(0))
                conv(s)

            def mix_channels(s, d=0):
                wait(pe, s_x1h, s.tile(1 + d))
                wait(pe, s_x1l, s.tile(1 + d))
                wait(pe, s_aggl, s.tile(1 + d))
                if s.there(1):
                    wait(pe, s_y32, s.tile(2 + d))
                mixing()

            def prelude():
                pe.wait_ge(s_cond, 16 * 2)
                nc.tensor.matmul(gat[0:NB, 128:128 + CH], embt[:, :], cwt[:, :], start=True, stop=True)\
                    .then_inc(s_row_mm, 1)
                pe.wait_ge(s_mlp, 16 * 2)
                nc.tensor.matmul(hwt[:, 0:NB], mw0[:, :], embt[:, :], start=True, stop=True).then_inc(s_mlp_mm, 1)
                pe.wait_ge(s_row, 3)
                pe.wait_ge(s_const, 5)
                pe.wait_ge(s_mlp_act, 1)
                nc.tensor.matmul(gat[:, 0:NB], mw1[:, :], h1[:, :], start=True, stop=True).then_inc(s_mlp_mm, 1)
                spread(0)
                pe.wait_ge(s_mlp_act, 2)
                nc.tensor.matmul(hwt[0:NB, 256:256 + NK], h2[:, :], mw2[:, :], start=True, stop=True)\
                    .then_inc(s_mlp_mm, 1)

            def attention():
                pe.wait_ge(s_mlp_dve, 6)
                nc.tensor.transpose(hwt[0:3 * NK, 256:256 + NB], att[:, :, :].rearrange("b s k -> b (s k)"),
                                    ident[0:NB, 0:NB]).then_inc(s_mlp_mm, 1)

            def bias_rows():
                pe.wait_ge(s_mlp_dve, 7)
                pe.wait_ge(s_kern3, 16 * 3)
                nc.tensor.matmul(hwt[0:NB, 128:128 + CH], attt[:, :], kern3[:, CH * CH:], start=True, stop=True)\
                    .then_inc(s_row_mm, 1)

            def aggregate(r):
                if r == 0:
                    pe.wait_ge(s_bcast_out, 2)
                else:
                    pe.wait_ge(s_agg_out, r)
                for o in range(16):
                    c = 32 * r + 2 * o
                    m = nc.tensor.matmul(acc[1][:, o * NB:(o + 1) * NB],
                                         kern3[:, c * CH:(c + 2) * CH], attt[:, :],
                                         start=True, stop=True)
                m.then_inc(s_agg, 1)

            def body(s):
                if s.is_tile(-1):
                    prelude()
                if s.there(0):
                    wait(pe, s_yh, s.tile(1))
                    wait(pe, s_yl, s.tile(1))
                    if s.is_tile(0):
                        for k in range(KT):
                            pe.wait_ge(s_split_h, k + 1)
                            pe.wait_ge(s_split_l, k + 1)
                            m = gates(0, yh, yl, G0W, k)
                            if k < KT - 2:
                                base(0, yh, yl, k)
                            if k == 0:
                                bias_rows()
                            if k == 1:
                                spread(1)
                            if k == 2:
                                aggregate(0)
                        m.then_inc(s_g[0], 1)
                        for k in range(KT - 2, KT):
                            base(0, yh, yl, k)
                        next_conv(s)
                        pe.wait_ge(s_split_l, LAYER0)
                    else:
                        for k in range(KT):
                            m = gates(0, yh, yl, G0W, k)
                        m.then_inc(s_g[0], 1)
                        if spreads(s):
                            spread(2 * s.tile())
                        if s.is_tile(1):
                            pe.wait_ge(s_x1, 1)
                        for k in range(KT):
                            if s.is_tile(1) and k == 2:
                                mix_channels(s, -1)
                            if k == KT - 1 and not s.there(1):
                                turn_hw(s, 0)
                            base(0, yh, yl, k)
                    if s.there(1):
                        turn_hw(s, 0)
                    if s.is_tile(0):
                        aggregate(1)
                if spreads(s):
                    spread(2 * s.tile() + 1)
                if s.there(1) and not s.is_tile(0):
                    if s.is_tile(0, 1):
                        pe.wait_ge(s_toep_l, 1)
                    next_conv(s)
                if s.is_tile(-1):
                    attention()
                if s.there(0):
                    wait(pe, s_hth[0], s.tile(1))
                    wait(pe, s_htl[0], s.tile(1))
                    lora_b(0)
                if s.there(-1):
                    wait(pe, s_zh, s.tile(0))
                    wait(pe, s_zl, s.tile(0))
                    if s.is_tile(0, -1):
                        order = [k % KT for k in range(5, 5 + KT)]
                        covering = order[-3:]
                        for k in order:
                            piece = LAYER0 + k - 5 if k >= 5 else LAYER0 + 4 + k
                            pe.wait_ge(s_split_h, piece + 1)
                            pe.wait_ge(s_split_l, piece + 1)
                            m = gates(1, zh, zl, G1W, k, order[0], order[-1])
                            if k not in covering:
                                if k == order[0]:
                                    pe.wait_ge(s_bcast_out, 4)
                                base(1, zh, zl, k, order[0])
                        m.then_inc(s_g[1], 1)
                    else:
                        covering = range(KT)
                        for k in range(KT):
                            m = gates(1, zh, zl, G1W, k)
                        m.then_inc(s_g[1], 1)
                        wait(pe, s_o, s.tile(-1))
                        if spreads(s):
                            pe.wait_ge(s_bcast_out, 2 * s.tile() + 2)
                    for k in covering:
                        if k == KT - 2 and s.is_tile(TILES - 1):
                            mix_channels(s)
                        if k == KT - 1 and not s.there(0):
                            turn_hw(s, 1)
                        base(1, zh, zl, k, 5 if s.is_tile(1) else 0)
                    if s.there(0):
                        turn_hw(s, 1)
                if s.there(0) and not s.is_tile(0) and not s.is_tile(TILES - 1):
                    mix_channels(s)
                if s.there(-1):
                    wait(pe, s_hth[1], s.tile(0))
                    wait(pe, s_htl[1], s.tile(0))
                    lora_b(1)

            pipeline(pe, body, TILES // 2 - 1, (-1, 3))


def kernel(**inputs):
    import numpy as _np
    import concourse.bacc as _bacc
    from concourse import mybir as _mybir
    from concourse.bass_utils import run_bass_kernel_spmd as _run

    a = {k: _np.asarray(v) for k, v in inputs.items()}
    w0 = _np.concatenate([a["L0_ffn_W_base"], a["L0_ffn_lora_A"].reshape(ER, L), a["L0_ffn_W_router"]])
    w1 = _np.concatenate([a["L1_ffn_W_base"], a["L1_ffn_A_w"].reshape(ER, L), a["L1_ffn_W_gate"],
                          a["L1_ffn_W_thr"].reshape(1, L)])
    args = [
        ("x", a["x"].reshape(NB * CH, L)),
        ("cond_t", _np.concatenate([a["cond_128"].T, a["L0_cond_c_weight"].T], axis=1)),
        ("fside", a["fside_S_0"]),
        ("conv_w", _np.pad(a["L0_cond_weight"].transpose(1, 2, 0), ((0, 0), (PH - 1, PH - 1), (0, 0)))),
        ("w_l0", w0.reshape(L + G0W, P, PH)[:, :, ::-1].transpose(1, 2, 0)),
        ("lora_b0", a["L0_ffn_lora_B"].transpose(0, 2, 1).reshape(ER, L)),
        ("b_l0", a["L0_ffn_b_base"]),
        ("mlp_w", _np.concatenate([a["L1_cond_W0"], a["L1_cond_W1"], a["L1_cond_W2"],
                                   a["L1_cond_b0"][:, None], a["L1_cond_b1"][:, None]], axis=1)),
        ("mlp_b2", a["L1_cond_b2"]),
        ("kern", _np.concatenate([a["L1_cond_weight"].reshape(NK, CH * CH), a["L1_cond_bias_k"]], axis=1)
         .reshape(P, KROW // 16)),
        ("w_l1", w1.reshape(L + G1W, KT, P).transpose(2, 1, 0)),
        ("lora_b1", a["L1_ffn_B_w"].transpose(0, 2, 1).reshape(ER, L)),
        ("b_l1", a["L1_ffn_b_base"]),
        ("b_thr", a["L1_ffn_b_thr"]),
    ]
    nc = _bacc.Bacc("TRN2", target_bir_lowering=False, num_devices=1)
    arrays, aps = {}, {}
    for name, v in args:
        v = _np.ascontiguousarray(v)
        arrays[f"{name}_dram"] = v
        aps[name] = nc.dram_tensor(f"{name}_dram", v.shape, _mybir.dt.from_np(v.dtype), kind="ExternalInput").ap()
    aps["out"] = nc.dram_tensor("out_dram", (NB * CH, L), _mybir.dt.float32, kind="ExternalOutput").ap()
    adaln_ffn(nc, **aps)
    r = _run(nc, [arrays], core_ids=[0])
    return r.results[0]["out_dram"].reshape(NB, CH, L)
```
